# Optimizing a Trainium2 kernel written in Bass

```python
import numpy as np
import jax
import jax.numpy as jnp

def _softmax(x, axis=-1):
    return jax.nn.softmax(x, axis=axis)

def _gelu(x):
    return jax.nn.gelu(x, approximate=True)

def _silu(x):
    return jax.nn.silu(x)

def _sigmoid(x):
    return jax.nn.sigmoid(x)

def _layernorm(x, axis=-1, eps=1e-05):
    m = jnp.mean(x, axis=axis, keepdims=True)
    v = jnp.var(x, axis=axis, keepdims=True)
    return (x - m) / jnp.sqrt(v + eps)

def _scatter_add(tgt, idx, src, axis=0):
    return tgt.at[idx].add(src)

def _segment_sum(src, seg, n):
    return jax.ops.segment_sum(src, seg, n)
kernel_name = 'mk_flamingo_gated_d1_seqx_r8_1472a2'

def setup_inputs(seed: int=0):
    np.random.seed(seed)
    _w = jnp.asarray

    def _rec_inputs():
        import jax
        import jax.numpy as jnp
        _rk = jax.random.key(seed)
        x = 7.22e-05 + 1 * jax.random.normal(jax.random.fold_in(_rk, 1), (4, 256, 256), jnp.float32)
        _lenS = 256 - jax.random.randint(jax.random.fold_in(_rk, 7), (4,), 0, max(1, 256 // 4) + 1, jnp.int32)
        _lenS2 = 1601 - jax.random.randint(jax.random.fold_in(_rk, 8), (4,), 0, max(1, 1601 // 4) + 1, jnp.int32)
        _ctx_2048P = jax.random.normal(jax.random.fold_in(_rk, 11), (4, 16, 256), jnp.float32)
        _ctx_2048c = jax.random.dirichlet(jax.random.fold_in(_rk, 511), 0.3 * jnp.ones((16,), jnp.float32), (4, 1601))
        _ctx_2048t = jnp.einsum('bsk,bkd->bsd', _ctx_2048c, _ctx_2048P)
        _ctx_2048t = _ctx_2048t * jax.lax.rsqrt(jnp.mean(jnp.square(_ctx_2048t)) + 1e-12) * 0.953939
        ctx_2048 = -0.000514642 + 1.00011 * (_ctx_2048t + 0.3 * jax.random.normal(jax.random.fold_in(_rk, 611), (4, 1601, 256), jnp.float32))
        _g = jax.random.normal(jax.random.fold_in(_rk, 9001), (2, 1), jnp.float32)
        _g = jnp.sign(_g) * jnp.maximum(jnp.abs(_g), 1.0) + (_g == 0) * 1.0
        g_xattn = _g[0]
        g_ffn = _g[1]
        return (x, ctx_2048, g_xattn, g_ffn)
    x, ctx_2048, g_xattn, g_ffn = _rec_inputs()

    def _L0_xattn_setup():
        import jax, jax.numpy as jnp
        import numpy as np
        D_MODEL = 256
        NUM_HEADS = 16
        HEAD_DIM = D_MODEL // NUM_HEADS

        def _fq_sym(x, axis):
            s = jnp.max(jnp.abs(x), axis=axis, keepdims=True) / 127.0
            s = jnp.maximum(s, 1e-08)
            q = jnp.clip(jnp.round(x / s), -127.0, 127.0) * s
            return x + jax.lax.stop_gradient(q - x)

        def _fq_unsigned(x, axis):
            s = jnp.max(x, axis=axis, keepdims=True) / 255.0
            s = jnp.maximum(s, 1e-08)
            q = jnp.clip(jnp.round(x / s), 0.0, 255.0) * s
            return x + jax.lax.stop_gradient(q - x)
        key = jax.random.key(seed)
        ks = jax.random.split(key, 8)
        B, N, M, C = (2, 256, 64, D_MODEL)
        return {'x': jax.random.normal(ks[0], (B, N, C), jnp.float32), 'cond': jax.random.normal(ks[1], (B, M, C), jnp.float32), 'Wq': jax.random.normal(ks[2], (C, C), jnp.float32) * 0.02, 'bq': jnp.zeros((C,), jnp.float32), 'Wkv': jax.random.normal(ks[3], (C, 2 * C), jnp.float32) * 0.02, 'bkv': jnp.zeros((2 * C,), jnp.float32), 'Wp': jax.random.normal(ks[4], (C, C), jnp.float32) * 0.02, 'bp': jnp.zeros((C,), jnp.float32)}
    _L0_xattn_all = _L0_xattn_setup()
    _L0_xattn_in = {k: v for k, v in _L0_xattn_all.items() if k in ('Wq', 'bq', 'Wkv', 'bkv', 'Wp', 'bp')}
    del _L0_xattn_all

    def _L0_ffn_setup():
        import jax, jax.numpy as jnp
        import numpy as np
        from jax import lax
        B, S, H = (1, 256, 256)
        E, I, TOP_K = (64, 64, 8)
        SHARED_I = 64
        key = jax.random.key(seed)
        ks = jax.random.split(key, 8)
        sc = 0.02
        return {'hidden_states': jax.random.normal(ks[0], (B, S, H), jnp.float32), 'router_w': jax.random.normal(ks[1], (E, H), jnp.float32) * sc, 'gate_up_proj': jax.random.normal(ks[2], (E, 2 * I, H), jnp.float32) * sc, 'down_proj': jax.random.normal(ks[3], (E, H, I), jnp.float32) * sc, 'shared_gate_w': jax.random.normal(ks[4], (SHARED_I, H), jnp.float32) * sc, 'shared_up_w': jax.random.normal(ks[5], (SHARED_I, H), jnp.float32) * sc, 'shared_down_w': jax.random.normal(ks[6], (H, SHARED_I), jnp.float32) * sc, 'shared_expert_gate_w': jax.random.normal(ks[7], (1, H), jnp.float32) * sc}
    _L0_ffn_all = _L0_ffn_setup()
    _L0_ffn_in = {k: v for k, v in _L0_ffn_all.items() if k in ('router_w', 'gate_up_proj', 'down_proj', 'shared_gate_w', 'shared_up_w', 'shared_down_w', 'shared_expert_gate_w')}
    del _L0_ffn_all
    return {'x': x, 'ctx_2048': ctx_2048, 'g_xattn': g_xattn, 'g_ffn': g_ffn, 'L0_xattn_Wq': _L0_xattn_in['Wq'], 'L0_xattn_bq': _L0_xattn_in['bq'], 'L0_xattn_Wkv': _L0_xattn_in['Wkv'], 'L0_xattn_bkv': _L0_xattn_in['bkv'], 'L0_xattn_Wp': _L0_xattn_in['Wp'], 'L0_xattn_bp': _L0_xattn_in['bp'], 'L0_ffn_router_w': _L0_ffn_in['router_w'], 'L0_ffn_gate_up_proj': _L0_ffn_in['gate_up_proj'], 'L0_ffn_down_proj': _L0_ffn_in['down_proj'], 'L0_ffn_shared_gate_w': _L0_ffn_in['shared_gate_w'], 'L0_ffn_shared_up_w': _L0_ffn_in['shared_up_w'], 'L0_ffn_shared_down_w': _L0_ffn_in['shared_down_w'], 'L0_ffn_shared_expert_gate_w': _L0_ffn_in['shared_expert_gate_w']}

def reference(x, ctx_2048, g_xattn, g_ffn, L0_xattn_Wq, L0_xattn_bq, L0_xattn_Wkv, L0_xattn_bkv, L0_xattn_Wp, L0_xattn_bp, L0_ffn_router_w, L0_ffn_gate_up_proj, L0_ffn_down_proj, L0_ffn_shared_gate_w, L0_ffn_shared_up_w, L0_ffn_shared_down_w, L0_ffn_shared_expert_gate_w):
    import jax
    import jax.numpy as jnp

    def _L0_xattn_ref(x, cond, Wq, bq, Wkv, bkv, Wp, bp):
        import jax, jax.numpy as jnp
        import numpy as np
        D_MODEL = 256
        NUM_HEADS = 16
        HEAD_DIM = D_MODEL // NUM_HEADS

        def _fq_sym(x, axis):
            s = jnp.max(jnp.abs(x), axis=axis, keepdims=True) / 127.0
            s = jnp.maximum(s, 1e-08)
            q = jnp.clip(jnp.round(x / s), -127.0, 127.0) * s
            return x + jax.lax.stop_gradient(q - x)

        def _fq_unsigned(x, axis):
            s = jnp.max(x, axis=axis, keepdims=True) / 255.0
            s = jnp.maximum(s, 1e-08)
            q = jnp.clip(jnp.round(x / s), 0.0, 255.0) * s
            return x + jax.lax.stop_gradient(q - x)
        B, N, C = x.shape
        H, hd = (NUM_HEADS, HEAD_DIM)
        q = (x @ Wq + bq).reshape(1, B * N, H, hd)
        kv = (cond @ Wkv + bkv).reshape(1, -1, 2, H, hd)
        k, v = (kv[:, :, 0], kv[:, :, 1])
        scale = 1.0 / np.sqrt(hd).astype(np.float32)
        q = jnp.transpose(q * scale, (0, 2, 1, 3))
        k = jnp.transpose(k, (0, 2, 1, 3))
        v = jnp.transpose(v, (0, 2, 1, 3))
        q = _fq_sym(q, axis=-1)
        k = _fq_sym(k, axis=-1)
        v = _fq_sym(v, axis=2)
        attn = jnp.einsum('bhqd,bhkd->bhqk', q, k)
        attn = jax.nn.softmax(attn.astype(jnp.float32), axis=-1)
        attn = _fq_unsigned(attn, axis=-1)
        out = jnp.einsum('bhqk,bhkd->bhqd', attn, v)
        out = jnp.transpose(out, (0, 2, 1, 3)).reshape(B, N, C)
        return out @ Wp + bp

    def _L0_ffn_ref(hidden_states, router_w, gate_up_proj, down_proj, shared_gate_w, shared_up_w, shared_down_w, shared_expert_gate_w):
        import jax, jax.numpy as jnp
        import numpy as np
        from jax import lax
        B, S, H = (1, 256, 256)
        E, I, TOP_K = (64, 64, 8)
        SHARED_I = 64
        b, s, h_dim = hidden_states.shape
        h = hidden_states.reshape(-1, h_dim)
        T = h.shape[0]
        shared = jnp.dot(jax.nn.silu(jnp.dot(h, shared_gate_w.T)) * jnp.dot(h, shared_up_w.T), shared_down_w.T)
        shared = jax.nn.sigmoid(jnp.dot(h, shared_expert_gate_w.T)) * shared
        logits = jnp.dot(h, router_w.T)
        probs = jax.nn.softmax(logits.astype(jnp.float32), axis=-1)
        top_vals, top_idx = lax.top_k(probs, TOP_K)
        top_vals = top_vals / jnp.sum(top_vals, axis=-1, keepdims=True)
        top_vals = top_vals.astype(h.dtype)
        comb = jnp.zeros((T, E), h.dtype).at[jnp.arange(T)[:, None], top_idx].add(top_vals)

        def body(acc, xs):
            wgu, wd, w_e = xs
            g, u = jnp.split(jnp.dot(h, wgu.T), 2, axis=-1)
            eo = jnp.dot(jax.nn.silu(g) * u, wd.T)
            return (acc + eo * w_e[:, None], None)
        expert_out, _ = lax.scan(body, jnp.zeros_like(h), (gate_up_proj, down_proj, comb.T))
        return (expert_out + shared).reshape(b, s, h_dim)
    x = x + jnp.tanh(g_xattn[0]) * _L0_xattn_ref(_layernorm(x, axis=-1), ctx_2048, L0_xattn_Wq, L0_xattn_bq, L0_xattn_Wkv, L0_xattn_bkv, L0_xattn_Wp, L0_xattn_bp)
    x = x + jnp.tanh(g_ffn[0]) * _L0_ffn_ref(_layernorm(x, axis=-1), L0_ffn_router_w, L0_ffn_gate_up_proj, L0_ffn_down_proj, L0_ffn_shared_gate_w, L0_ffn_shared_up_w, L0_ffn_shared_down_w, L0_ffn_shared_expert_gate_w)
    return x

_drawn_inputs = setup_inputs


def setup_inputs(seed=0):
    import zlib

    import numpy as np

    out = dict(_drawn_inputs(seed))
    spreads = {'L0_xattn_bq': (0.0, 0.8), 'L0_xattn_bkv': (0.0, 0.317), 'L0_xattn_bp': (0.0, 0.1)}
    factors = {'ctx_2048': 3.148,
     'L0_xattn_Wq': 8.0,
     'L0_xattn_Wkv': 3.095,
     'L0_ffn_router_w': 8.0,
     'L0_ffn_gate_up_proj': 8.0,
     'L0_ffn_down_proj': 8.0,
     'L0_ffn_shared_gate_w': 8.0,
     'L0_ffn_shared_up_w': 8.0,
     'L0_ffn_shared_down_w': 8.0,
     'L0_ffn_shared_expert_gate_w': 8.0}
    for name, (base, spread) in spreads.items():
        noise = np.random.default_rng([zlib.crc32(name.encode()), seed]).standard_normal(out[name].shape)
        drawn = base * np.exp(spread * noise) if base else spread * noise
        out[name] = jnp.asarray(drawn.astype(out[name].dtype))
    for name, factor in factors.items():
        out[name] = (out[name] * factor).astype(out[name].dtype)
    return out
```

```python
from contextlib import ExitStack

import concourse.bass as bass
from concourse import mybir

F32 = mybir.dt.float32
BF16 = mybir.dt.bfloat16
U8 = mybir.dt.uint8
U32 = mybir.dt.uint32
ALU = mybir.AluOpType
ACT = mybir.ActivationFunctionType
AX = mybir.AxisListType

P = 128
D = 256
KD = D // P
H = 16
HD = D // H
NQ = 1024
QT = NQ // P
NK = 6404
KC = 512
NKC = NK // KC
TAIL = NK - NKC * KC
TAILW = TAIL // 4
VT = 4 * (NKC + 1)
PARTS = 3
QR = PARTS * HD
HP = 64
SC = 1024
SCS = [(a, min(SC, NK - a)) for a in range(0, NK, SC)]
NSC = len(SCS)
UNITS = H * QT
STEPS = UNITS // 2
WG = 4
E = 64
I = 64
EG = 4
NEG = E // EG
TOPK = 8
ROUND = 1.5 * 2.0 ** 23
LN255 = 5.541263545158426
LN_EPS = 1e-5
QMIN = 1e-8


def last_axis(ap, n):
    return ap.unsqueeze(len(ap.shape)).broadcast_to(list(ap.shape) + [n])


def middle_axis(ap, n):
    return ap.unsqueeze(1).broadcast_to([ap.shape[0], n, ap.shape[1]])


class Steps:

    def __init__(self, engine, sem, base=0):
        self.engine, self.sem, self.n, self.base = engine, sem, 0, base

    def then(self, instruction):
        instruction.then_inc(self.sem, 1)
        self.n += 1
        self.engine.wait_ge(self.sem, self.base + self.n)


LN_STEPS = 8
BEFORE_LN = 4
VAR_STEP = 3


def layernorm(nc, dve, steps, x, stats, mv, ln, out, root, ready):
    for t in range(QT):
        done = nc.vector.bn_stats(stats[:, t, :], x[:, t, :])
    steps.then(done)
    for t in range(QT):
        done = nc.vector.bn_aggr(mv[:, t, :], stats[:, t, :])
    steps.then(done)
    steps.then(nc.vector.tensor_scalar(ln[:, 0, :], mv[:, :, 1], LN_EPS, None, ALU.add))
    assert steps.n == VAR_STEP
    dve.wait_ge(root, 1)
    steps.then(nc.vector.reciprocal(ln[:, 2, :], ln[:, 1, :]))
    steps.then(nc.vector.tensor_tensor(ln[:, 3, :], ln[:, 0, :], ln[:, 2, :], ALU.mult))
    steps.then(nc.vector.tensor_tensor(ln[:, 3, :], ln[:, 3, :], ln[:, 2, :], ALU.mult))
    steps.then(nc.vector.tensor_scalar(ln[:, 3, :], ln[:, 3, :], -0.5, 1.5, ALU.mult, ALU.add))
    steps.then(nc.vector.tensor_tensor(ln[:, 2, :], ln[:, 2, :], ln[:, 3, :], ALU.mult))
    for t in range(QT):
        done = nc.vector.tensor_scalar(out[:, t, :], x[:, t, :], mv[:, t, 0:1], ln[:, 2, t:t + 1],
                                       ALU.subtract, ALU.mult)
    done.then_inc(ready, 1)
    dve.wait_ge(ready, 1)
    assert steps.n == LN_STEPS


def projections(nc, io, keep, scratch):
    x, ident, sv = keep["x"], keep["ident"], keep["sv"]
    sq = keep["sq"]
    kT_d, qT_d, v_d = scratch
    with ExitStack() as ctx:
        def sb(name, shape, dt=F32):
            return ctx.enter_context(nc.sbuf_tensor(name, shape, dt))

        def psum(name, shape, dt=F32):
            return ctx.enter_context(nc.psum_tensor(name, shape, dt))

        def sem(name):
            return ctx.enter_context(nc.semaphore(name))

        identb = sb("identb", [P, P], BF16)
        ones = sb("ones", [P, P])
        wq = sb("wq", [P, KD, D])
        wkv = sb("wkv", [P, KD, 2 * D])
        bq = sb("bq", [P, D])
        bkv = sb("bkv", [P, 2 * D])
        stats = sb("stats", [P, QT, 6])
        mv = sb("mv", [P, QT, 2])
        ln = sb("ln", [P, 4, QT])
        h = sb("h", [P, QT, D])
        hT = sb("hT", [P, KD, NQ])
        ctxc = sb("ctxc", [P, 2, KD, KC])
        kf = sb("kf", [P, 4, D])
        kr = sb("kr", [P, 4, D])
        kq = sb("kq", [P, 2, 4, D])
        kres = sb("kres", [P, 4, D])
        amax = sb("amax", [P, 4 * H])
        kscale = sb("kscale", [P, 4 * H])
        kinv = sb("kinv", [P, 4 * H])
        parts = sb("parts", [P, 2, 4, H, HP], BF16)
        turned = sb("turned", [P, 2, H // 2, KC], BF16)
        vf = sb("vf", [P, VT, D])
        vmax = sb("vmax", [P, D])
        vcol = sb("vcol", [P, KD])
        vdiag = sb("vdiag", [P, KD, P])
        vinv = sb("vinv", [P, D])
        vr = sb("vr", [P, VT, 4 * HD])
        vint = sb("vint", [P, 2, 4, VT, HD], BF16)

        pk = psum("pk", [P, 4, D])
        pv = psum("pv", [P, 4, D])
        pt = psum("pt", [P, H // 2, KC], BF16)
        ptf = pt[:, :, :].rearrange("p a b -> p (a b)").bitcast(F32)

        loaded = sem("loaded")
        ctx_in = [sem("ctx_in0"), sem("ctx_in1")]
        consts = sem("consts")
        qsteps = sem("qsteps")
        root = sem("root")
        h_ready = sem("h_ready")
        hT_turned = sem("hT_turned")
        hT_ready = sem("hT_ready")
        q_ready = sem("q_ready")
        q_taken = sem("q_taken")
        qparts = sem("qparts")
        k_ready = sem("k_ready")
        v_ready = sem("v_ready")
        ksteps = sem("ksteps")
        k_taken = sem("k_taken")
        kq_ready = sem("kq_ready")
        v_taken = sem("v_taken")
        hi_done = sem("hi_done")
        res_done = sem("res_done")
        mid_done = sem("mid_done")
        kparts = sem("kparts")
        turned_ready = sem("turned_ready")
        turned_taken = sem("turned_taken")
        stored = [sem("stored0"), sem("stored1")]
        vsteps = sem("vsteps")
        v_turned = sem("v_turned")
        v_diag = sem("v_diag")
        v_bcast = sem("v_bcast")
        vint_ready = sem("vint_ready")
        v_stored = [sem("v_stored0"), sem("v_stored1")]

        block = ctx.enter_context(nc.Block())
        LK = 5
        ctx_view = io["ctxT"].rearrange("(k p) n -> p k n", p=P)

        @block.sync
        def _(sp):
            for dst, src in ((x[:, :, :], io["x"].rearrange("(t p) d -> p t d", p=P)),
                             (ident[:, :], io["eye"]),
                             (bq[:, :], io["bq"].broadcast_to([P, D])),
                             (bkv[:, :], io["bkv"].broadcast_to([P, 2 * D])),
                             (wq[:, :, :], io["Wq"].rearrange("(k p) n -> p k n", p=P)),
                             (wkv[:, :, :], io["Wkv"].rearrange("(k p) n -> p k n", p=P))):
                sp.dma_start(dst, src).then_inc(loaded, 16)

            def load(c, par, width):
                sp.dma_start(ctxc[:, par, :, 0:width],
                             ctx_view[:, :, bass.ds(c * KC, width)]).then_inc(ctx_in[par], 16)

            def store(n, par, dram, at, width):
                sp.wait_ge(turned_taken, n + 1)
                for half in range(2):
                    dst = dram.rearrange("(g two) r n -> two r g n", two=2)[half]
                    sp.dma_start(dst[:, :, bass.ds(at, width)],
                                 turned[HP * half:HP * half + QR, par, :, 0:width]).then_inc(stored[par], 16)

            load(0, 0, KC)
            load(1, 1, KC)
            for r in range(2):
                store(r, r, qT_d, r * KC, KC)
            with sp.Fori(0, NKC // 2 - 1) as i:
                for par in range(2):
                    c = 2 * i + par
                    sp.wait_ge(v_ready, c + 1)
                    load(c + 2, par, KC)
                    store(c + 2, par, kT_d, c * KC, KC)
            sp.wait_ge(v_ready, NKC - 1)
            load(NKC, 0, TAIL)
            store(NKC, 0, kT_d, (NKC - 2) * KC, KC)
            store(NKC + 1, 1, kT_d, (NKC - 1) * KC, KC)
            store(NKC + 2, 0, kT_d, NKC * KC, TAIL)
            for n in range(4):
                sp.wait_ge(vint_ready, n + 1)
                sp.dma_start(v_d.rearrange("h p n -> p h n")[:, 4 * n:4 * n + 4, :],
                             vint[:, n % 2].rearrange("p h t d -> p h (t d)")).then_inc(v_stored[n % 2], 16)
            sp.wait_ge(stored[0], 32 * (NKC // 2 + 2))
            sp.wait_ge(stored[1], 32 * (NKC // 2 + 1))
            for b in range(2):
                sp.wait_ge(v_stored[b], 32)

        @block.gpsimd
        def _(pool):
            pool.memset(ones[:, :], 1.0).then_inc(consts, 1)
            pool.memset(parts[:, :, :, :, :].rearrange("p a b h n -> p (a b h n)").bitcast(U32), 0).then_inc(consts, 1)
            pool.memset(vf[:, VT - 4:VT, :], 0.0).then_inc(consts, 1)

            def residuals(c, par):
                pool.wait_ge(hi_done, c + 1)
                if not (isinstance(c, int) and c == 0):
                    pool.wait_ge(kparts, c)
                pool.tensor_tensor(kres[:, :, :].rearrange("p i (h e) -> p i h e", h=H),
                                   kq[:, par].rearrange("p i (h e) -> p i h e", h=H),
                                   parts[:, par, :, :, 0:HD], ALU.subtract).then_inc(res_done, 1)
                pool.wait_ge(mid_done, c + 1)
                pool.tensor_tensor(parts[:, par, :, :, 2 * HD:3 * HD],
                                   kres[:, :, :].rearrange("p i (h e) -> p i h e", h=H),
                                   parts[:, par, :, :, HD:2 * HD], ALU.subtract).then_inc(kparts, 1)

            residuals(0, 0)
            residuals(1, 1)
            with pool.Fori(1, NKC // 2) as i:
                for par in range(2):
                    residuals(2 * i + par, par)
            residuals(NKC, 0)

        @block.scalar
        def _(act):
            act.wait_ge(qsteps, VAR_STEP)
            nc.scalar.activation(ln[:, 1, :], ln[:, 0, :], ACT.Sqrt).then_inc(root, 1)
            for k in range(KD):
                act.wait_ge(hT_turned, k + 1)
                nc.scalar.copy(hT[:, k, :], ptf[:, k * NQ:(k + 1) * NQ]).then_inc(hT_ready, 1)

            def first_parts(c, par):
                act.wait_ge(kq_ready, c + 1)
                act.wait_ge(turned_ready, c + 1)
                nc.scalar.copy(parts[:, par, :, :, 0:HD],
                               kq[:, par].rearrange("p i (h e) -> p i h e", h=H)).then_inc(hi_done, 1)

            def second_parts(c, par):
                act.wait_ge(res_done, c + 1)
                nc.scalar.copy(parts[:, par, :, :, HD:2 * HD],
                               kres[:, :, :].rearrange("p i (h e) -> p i h e", h=H)).then_inc(mid_done, 1)

            def evacuate_item(n, par, uses):
                act.wait_ge(turned_ready, n + 1)
                if not (isinstance(uses, int) and uses == 0):
                    act.wait_ge(stored[par], 32 * uses)
                nc.scalar.copy(turned[:, par, :, :], pt[:, :, :]).then_inc(turned_taken, 1)

            evacuate_item(0, 0, 0)
            first_parts(0, 0)
            evacuate_item(1, 1, 0)
            second_parts(0, 0)
            first_parts(1, 1)
            evacuate_item(2, 0, 1)
            second_parts(1, 1)
            with act.Fori(1, NKC // 2) as i:
                first_parts(2 * i, 0)
                evacuate_item(2 * i + 1, 1, i)
                second_parts(2 * i, 0)
                first_parts(2 * i + 1, 1)
                evacuate_item(2 * i + 2, 0, i + 1)
                second_parts(2 * i + 1, 1)
            first_parts(NKC, 0)
            evacuate_item(NKC + 1, 1, NKC // 2)
            second_parts(NKC, 0)
            evacuate_item(NKC + 2, 0, NKC // 2 + 1)

        @block.tensor
        def _(pe):
            pe.wait_ge(h_ready, 1)
            for k in range(KD):
                for t in range(QT):
                    mm = nc.tensor.transpose(ptf[:, k * NQ + t * P:k * NQ + (t + 1) * P],
                                             h[:, t, k * P:(k + 1) * P], ident[:, :])
                mm.then_inc(hT_turned, 1)
            pe.wait_ge(hT_ready, KD)
            for t in range(QT):
                out = (pk if t < 4 else pv)[:, t % 4, :]
                for k in range(KD):
                    mm = nc.tensor.matmul(out, hT[:, k, t * P:(t + 1) * P], wq[:, k, :],
                                          start=(k == 0), stop=(k == KD - 1))
            mm.then_inc(q_ready, 1)

            def turn(n, par):
                if not (isinstance(n, int) and n == 0):
                    pe.wait_ge(turned_taken, n)
                for i in range(4):
                    for g in range(H // 2):
                        mm = nc.tensor.transpose(
                            pt[:, g, i * P:(i + 1) * P],
                            parts[:, par, i, 2 * g:2 * g + 2, :].rearrange("p a b -> p (a b)"), identb[:, :])
                mm.then_inc(turned_ready, 1)

            def project(c, par, width, loads):
                pe.wait_ge(ctx_in[par], 16 * loads)
                if isinstance(c, int) and c == 0:
                    pe.wait_ge(q_taken, 2)
                else:
                    pe.wait_ge(k_taken, c)
                for i in range(-(-width // P)):
                    m = min(P, width - i * P)
                    for k in range(KD):
                        mm = nc.tensor.matmul(pk[0:m, i, :], ctxc[:, par, k, i * P:i * P + m], wkv[:, k, 0:D],
                                              start=(k == 0), stop=(k == KD - 1))
                mm.then_inc(k_ready, 1)
                if not (isinstance(c, int) and c == 0):
                    pe.wait_ge(v_taken, c)
                for b in range(4):
                    for k in range(KD):
                        mm = nc.tensor.matmul(pv[0:width // 4, b, :], ctxc[:, par, k, b:width:4], wkv[:, k, D:2 * D],
                                              start=(k == 0), stop=(k == KD - 1))
                mm.then_inc(v_ready, 1)

            project(0, 0, KC, 1)
            for r in range(2):
                pe.wait_ge(qparts, r + 1)
                turn(r, r)
            project(1, 1, KC, 1)
            pe.wait_ge(kparts, 1)
            turn(2, 0)
            with pe.Fori(1, NKC // 2) as i:
                for par in range(2):
                    project(2 * i + par, par, KC, i + 1)
                    pe.wait_ge(kparts, 2 * i + par)
                    turn(2 * i + par + 1, 1 - par)
            project(NKC, 0, TAIL, NKC // 2 + 1)
            for c in (NKC - 1, NKC):
                pe.wait_ge(kparts, c + 1)
                turn(c + 2, c % 2)

            pe.wait_ge(vsteps, 1)
            for k in range(KD):
                mm = nc.tensor.transpose(pk[:, 0, k * P:(k + 1) * P], vmax[:, k * P:(k + 1) * P], ident[:, :])
            mm.then_inc(v_turned, 1)
            pe.wait_ge(v_diag, 1)
            mm = nc.tensor.matmul(pk[:, 2, :], ones[:, :], vdiag[:, :, :].rearrange("p k n -> p (k n)"),
                                  start=True, stop=True)
            mm.then_inc(v_bcast, 1)

        @block.vector
        def _(dve):
            q = Steps(dve, qsteps)
            dve.wait_ge(loaded, 16 * 6)
            dve.wait_ge(consts, 3)
            nc.vector.tensor_copy(identb[:, :], ident[:, :])
            layernorm(nc, dve, q, x, stats, mv, ln, h, root, h_ready)
            dve.wait_ge(q_ready, 1)
            for r, bank in enumerate((pk, pv)):
                nc.vector.tensor_tensor(kf[:, :, :], bank[:, :, :], middle_axis(bq[:, :], 4),
                                        ALU.add).then_inc(q_taken, 1)
                dve.wait_ge(q_taken, r + 1)
                q.then(nc.vector.tensor_reduce(amax[:, :], kf[:, :, :].rearrange("p i (h e) -> p (i h) e", e=HD),
                                               AX.X, ALU.max, apply_absolute_value=True))
                q.then(nc.vector.tensor_scalar(kscale[:, :], amax[:, :], 1.0 / 127.0, 4 * QMIN, ALU.mult, ALU.max))
                q.then(nc.vector.reciprocal(kinv[:, :], kscale[:, :]))
                nc.vector.tensor_scalar(
                    sq[:, 2 * r * H:2 * (r + 1) * H, :].rearrange("p (g h) j -> p g h j", h=H),
                    kscale[:, :].rearrange("p (g j h) -> p g h j", g=2, j=2), 0.25, None, ALU.mult)
                q.then(nc.vector.tensor_tensor(kr[:, :, :].rearrange("p i (h e) -> p (i h) e", e=HD),
                                               kf[:, :, :].rearrange("p i (h e) -> p (i h) e", e=HD),
                                               last_axis(kinv[:, :], HD), ALU.mult))
                for part in range(PARTS):
                    done = nc.vector.tensor_scalar(
                        parts[:, r, :, :, part * HD:(part + 1) * HD].rearrange("p i h e -> p (i h) e"),
                        kr[:, :, :].rearrange("p i (h e) -> p (i h) e", e=HD), ROUND, ROUND, ALU.add, ALU.subtract)
                done.then_inc(qparts, 1)
                dve.wait_ge(qparts, r + 1)

            def quantise(c, par, rows):
                k = Steps(dve, ksteps, LK * c)
                dve.wait_ge(k_ready, c + 1)
                heads = lambda t: t.rearrange("p i (h e) -> p (i h) e", e=HD)
                nc.vector.tensor_tensor(kf[:, :, :], pk[:, :, :], middle_axis(bkv[:, 0:D], 4),
                                        ALU.add).then_inc(k_taken, 1)
                dve.wait_ge(k_taken, c + 1)
                k.then(nc.vector.tensor_reduce(amax[:, :], heads(kf[:, :, :]), AX.X, ALU.max,
                                               apply_absolute_value=True))
                k.then(nc.vector.tensor_scalar(kscale[:, :], amax[:, :], 1.0 / 127.0, QMIN, ALU.mult, ALU.max))
                k.then(nc.vector.reciprocal(kinv[:, :], kscale[:, :]))
                k.then(nc.vector.tensor_tensor(heads(kr[:, :, :]), heads(kf[:, :, :]), last_axis(kinv[:, :], HD),
                                               ALU.mult))
                k.then(nc.vector.tensor_scalar(kr[:, :, :], kr[:, :, :], ROUND, ROUND, ALU.add, ALU.subtract))
                if not (isinstance(c, int) and c < 2):
                    dve.wait_ge(res_done, c - 1)
                nc.vector.tensor_tensor(heads(kq[:, par]), heads(kr[:, :, :]), last_axis(kscale[:, :], HD),
                                        ALU.mult).then_inc(kq_ready, 1)
                dve.wait_ge(v_ready, c + 1)
                nc.vector.tensor_tensor(vf[0:rows, bass.ds(4 * c, 4), :], pv[0:rows, :, :],
                                        middle_axis(bkv[0:rows, D:2 * D], 4), ALU.add).then_inc(v_taken, 1)

            quantise(0, 0, P)
            quantise(1, 1, P)
            with dve.Fori(1, NKC // 2) as i:
                for par in range(2):
                    quantise(2 * i + par, par, P)
            quantise(NKC, 0, TAILW)

            v = Steps(dve, vsteps)
            dve.wait_ge(v_taken, NKC + 1)
            v.then(nc.vector.tensor_reduce(vmax[:, :], vf[:, :, :].rearrange("p t d -> p d t"), AX.X, ALU.max,
                                           apply_absolute_value=True))
            dve.wait_ge(v_turned, 1)
            v.then(nc.vector.tensor_reduce(vcol[:, :], pk[:, 0, :].rearrange("p (k n) -> p k n", k=KD), AX.X, ALU.max))
            for k in range(KD):
                done = nc.vector.tensor_scalar(vdiag[:, k, :], ident[:, :], vcol[:, k:k + 1], None, ALU.mult)
            done.then_inc(v_diag, 1)
            dve.wait_ge(v_bcast, 1)
            v.then(nc.vector.tensor_scalar(sv[:, :], pk[:, 2, :], 1.0 / 127.0, QMIN, ALU.mult, ALU.max))
            v.then(nc.vector.reciprocal(vinv[:, :], sv[:, :]))
            for n in range(4):
                cols = slice(4 * n * HD, 4 * (n + 1) * HD)
                v.then(nc.vector.tensor_tensor(vr[:, :, :], vf[:, :, cols], middle_axis(vinv[:, cols], VT), ALU.mult))
                if n >= 2:
                    dve.wait_ge(v_stored[n % 2], 16)
                for hh in range(4):
                    done = nc.vector.tensor_scalar(vint[:, n % 2, hh], vr[:, :, hh * HD:(hh + 1) * HD],
                                                   ROUND, ROUND, ALU.add, ALU.subtract)
                done.then_inc(vint_ready, 1)
                dve.wait_ge(vint_ready, n + 1)


def attention(nc, keep, scratch):
    ident, sq, o, sums = keep["ident"], keep["sq"], keep["o"], keep["sums"]
    kT_d, qT_d, v_d = scratch
    LAG_T, LAG_PV = 2, 4
    with ExitStack() as ctx:
        def sb(name, shape, dt=F32):
            return ctx.enter_context(nc.sbuf_tensor(name, shape, dt))

        def psum(name, shape, dt=F32):
            return ctx.enter_context(nc.psum_tensor(name, shape, dt))

        def sem(name):
            return ctx.enter_context(nc.semaphore(name))

        kT = sb("kT", [P, 2, NK], BF16)
        qT = sb("qT", [P, 2, 2 * P], BF16)
        v = sb("v_head", [P, 2, VT, HD], BF16)
        s = sb("s", [P, 2, NK])
        e8 = sb("e8", [P, 2, NK], U8)
        words = sb("words", [P, 2, NKC + 1, P], U32)
        pT = sb("pT", [P, 2, VT, P], BF16)
        smax = sb("smax", [P, 2, NSC])
        nmax = sb("nmax", [P, 2])
        bias = sb("bias", [P, 2])

        ps = psum("ps", [P, 2, SC])
        pw = psum("pw", [P, 3, KC])
        po = psum("po", [P, KC])

        heads_in = [sem("heads_in0"), sem("heads_in1")]
        v_in = [sem("v_in0"), sem("v_in1")]
        const = sem("const")
        scored = sem("scored")
        copied = sem("copied")
        bias_ready = sem("bias_ready")
        exped = sem("exped")
        turned = sem("turned")
        wordsd = sem("wordsd")
        unpacked = sem("unpacked")
        weighed = sem("weighed")
        o_taken = sem("o_taken")
        pool_passed = sem("pool_passed")
        max_ready = sem("max_ready")

        sqf = sq[:, :, :].rearrange("p s j -> p (s j)")

        block = ctx.enter_context(nc.Block())

        def first(n):
            return isinstance(n, int) and n < 2

        @block.sync
        def _(sp):
            def load_heads(st, par, head, group):
                if not first(st):
                    sp.wait_ge(scored, 2 * NSC * (st - 1))
                sp.dma_start(kT[0:QR, par, :],
                             kT_d[bass.ds(head, 1)].rearrange("o r n -> (o r) n")).then_inc(heads_in[par], 16)
                sp.dma_start(qT[0:QR, par, :],
                             qT_d[bass.ds(head, 1), :, bass.ds(group * 2 * P, 2 * P)]
                             .rearrange("o r n -> (o r) n")).then_inc(heads_in[par], 16)

            def load_v(st, par, head):
                if not first(st):
                    sp.wait_ge(weighed, 2 * (st - 1))
                sp.dma_start(v[:, par].rearrange("p t d -> p (t d)"),
                             v_d[bass.ds(head, 1)].rearrange("o p n -> (o p) n")).then_inc(v_in[par], 16)

            sp.wait_ge(const, 2)
            load_heads(0, 0, 0, 0)
            load_heads(1, 1, 1, 0)
            load_v(0, 0, 0)
            load_heads(2, 0, 2, 0)
            load_v(1, 1, 1)
            load_heads(3, 1, 3, 0)
            load_v(2, 0, 2)
            with sp.Fori(2, STEPS // 2) as i:
                group, hp = i // (H // 2), i % (H // 2)
                load_heads(2 * i, 0, 2 * hp, group)
                load_v(2 * i - 1, 1, (2 * hp + H - 1) % H)
                load_heads(2 * i + 1, 1, 2 * hp + 1, group)
                load_v(2 * i, 0, 2 * hp)
            load_v(STEPS - 1, 1, H - 1)
            for par in range(2):
                sp.wait_ge(heads_in[par], 32 * (STEPS // 2))
                sp.wait_ge(v_in[par], 16 * (STEPS // 2))

        @block.tensor
        def _(pe):
            def scores(u, par, j, early, c):
                a, w = SCS[c]
                n = NSC * u + c
                if not (early and u == 0 and c < 2):
                    pe.wait_ge(copied, n - 1)
                for b in range(a, a + w, KC):
                    m = min(KC, a + w - b)
                    mm = nc.tensor.matmul(ps[:, c_buf(par, j, c), b - a:b - a + m], qT[:, par, j * P:(j + 1) * P],
                                          kT[:, par, b:b + m], start=True, stop=True)
                mm.then_inc(scored, 1)

            def c_buf(par, j, c):
                return (NSC * j + c) % 2

            def turn(w_, j, g, early):
                if g == 0 and not early:
                    pe.wait_ge(wordsd, WG * w_)
                if g == 0:
                    pe.wait_ge(exped, w_ + 1)
                if g == WG - 1:
                    pe.wait_ge(wordsd, WG * w_ + 1)
                ew = e8[:, j, :].bitcast(F32)
                for t in range(4 * g, min(4 * g + 4, NKC + 1)):
                    m = min(P, NK // 4 - t * P)
                    mm = nc.tensor.transpose(pw[0:m, g % 3, (t % 4) * P:(t % 4 + 1) * P], ew[:, t * P:t * P + m],
                                             ident[:, :])
                mm.then_inc(turned, 1)

            def weigh(w_, par, j, g, early):
                if g == 0:
                    pe.wait_ge(v_in[par], vcount(w_))
                    if not (early and w_ == 0):
                        pe.wait_ge(o_taken, w_)
                pe.wait_ge(unpacked, WG * w_ + g + 1)
                last = min(16 * g + 16, VT)
                for t in range(16 * g, last):
                    m = min(P, NK // 4 - (t // 4) * P)
                    mm = nc.tensor.matmul(po[:, 0:HD], pT[0:m, j, t, :], v[0:m, par, t, :],
                                          start=(t == 0), stop=(t == VT - 1))
                if g == WG - 1:
                    mm.then_inc(weighed, 1)

            loads = [0]

            def vcount(w_):
                return loads[0]

            def unit(u, i, par, j, early):
                k = 2 * par + j
                t_on = not early or k >= LAG_T
                if j == 0:
                    pe.wait_ge(heads_in[par], 32 * (i + 1))
                for c in range(NSC):
                    scores(u, par, j, early, c)
                    if t_on and c in (1, 2, 3):
                        turn(u - LAG_T, j, c - 1, early and k == LAG_T)
                    if not early:
                        loads[0] = 16 * i
                        if c in (2, 3, 4, 5):
                            weigh(u - LAG_PV, par, j, c - 2, early_pv[0] and k == 0)
                if t_on:
                    turn(u - LAG_T, j, WG - 1, False)

            early_pv = [False]
            for k in range(4):
                unit(k, 0, k // 2, k % 2, True)
            early_pv[0] = True
            for k in range(4):
                unit(4 + k, 1, k // 2, k % 2, False)
            early_pv[0] = False
            with pe.Fori(2, UNITS // 4) as i:
                for k in range(4):
                    unit(4 * i + k, i, k // 2, k % 2, False)
            for k in range(4):
                u = UNITS + k
                loads[0] = 16 * (STEPS // 2)
                if k < LAG_T:
                    for g in range(3):
                        turn(u - LAG_T, k % 2, g, False)
                for g in range(WG):
                    weigh(u - LAG_PV, k // 2, k % 2, g, False)
                if k < LAG_T:
                    turn(u - LAG_T, k % 2, WG - 1, False)

        @block.scalar
        def _(act):
            def exp(u, j, early):
                act.wait_ge(bias_ready, u + 1)
                if not early:
                    act.wait_ge(turned, WG * (u - 1))
                nc.scalar.activation(e8[:, j, :], s[:, j, :], ACT.Exp, bias=bias[:, j:j + 1],
                                     scale=sqf[:, bass.ds(u, 1)], accum_out=sums[:, bass.ds(u, 1)]).then_inc(exped, 1)

            def take_words(w_, j, early):
                if not early:
                    act.wait_ge(unpacked, WG * (w_ - 1))
                for g in range(WG):
                    act.wait_ge(turned, WG * w_ + g + 1)
                    if g < WG - 1:
                        nc.scalar.copy(words[:, j, 4 * g:4 * g + 4, :].rearrange("p t q -> p (t q)"),
                                       pw[:, g, :].bitcast(U32)).then_inc(wordsd, 1)
                    else:
                        nc.scalar.copy(words[0:TAILW, j, NKC, :], pw[0:TAILW, 0, 0:P].bitcast(U32)).then_inc(wordsd, 1)

            exp(0, 0, True)
            exp(1, 1, True)
            take_words(0, 0, True)
            exp(2, 0, False)
            take_words(1, 1, True)
            exp(3, 1, False)
            with act.Fori(2, UNITS // 2) as i:
                for j in range(2):
                    take_words(2 * i + j - 2, j, False)
                    exp(2 * i + j, j, False)
            for j in range(2):
                take_words(UNITS - 2 + j, j, False)

        @block.gpsimd
        def _(pool):
            def unpack(w_, j, early):
                if not early:
                    pool.wait_ge(weighed, w_ - 1)
                for g in range(WG):
                    pool.wait_ge(wordsd, WG * w_ + g + 1)
                    pool.sem_inc(pool_passed, 1)
                    m, a, b = (P, 4 * g, 4 * g + 4) if g < WG - 1 else (TAILW, NKC, NKC + 1)
                    nc.gpsimd.tensor_scalar(
                        pT[0:m, j, 4 * a:4 * b, :].rearrange("p (t b) q -> p t b q", b=4),
                        words[0:m, j, a:b, :].bitcast(U8).rearrange("p t (q b) -> p t b q", b=4),
                        1.0, 0.0, ALU.mult, ALU.add).then_inc(unpacked, 1)

            unpack(0, 0, True)
            unpack(1, 1, True)
            with pool.Fori(1, UNITS // 2) as i:
                for j in range(2):
                    unpack(2 * i + j, j, False)

        @block.vector
        def _(dve):
            nc.vector.memset(kT[:, :, :].rearrange("p a n -> p (a n)").bitcast(U32), 0).then_inc(const, 1)
            nc.vector.memset(qT[:, :, :].rearrange("p a n -> p (a n)").bitcast(U32), 0).then_inc(const, 1)

            def take_o(w_):
                dve.wait_ge(weighed, w_ + 1)
                nc.vector.tensor_copy(o[:, bass.ds(w_ * HD, HD)], po[:, 0:HD]).then_inc(o_taken, 1)

            def unit(u, j, early):
                if not (early and u < 2):
                    dve.wait_ge(exped, u - 1)
                for c, (a, w) in enumerate(SCS):
                    dve.wait_ge(scored, NSC * u + c + 1)
                    nc.vector.tensor_scalar(s[:, j, a:a + w], ps[:, (NSC * j + c) % 2, 0:w], 1.0, None,
                                            ALU.mult, ALU.max, accum_out=smax[:, j, c:c + 1]).then_inc(copied, 1)
                    if c == 1 and not (early and u <= LAG_PV):
                        take_o(u - LAG_PV - 1)
                dve.wait_ge(copied, NSC * (u + 1))
                nc.vector.tensor_reduce(nmax[:, j:j + 1], smax[:, j, :], AX.X, ALU.max, negate=True).then_inc(max_ready, 1)
                dve.wait_ge(max_ready, u + 1)
                nc.vector.tensor_scalar(bias[:, j:j + 1], nmax[:, j:j + 1], sqf[:, bass.ds(u, 1)], LN255,
                                        ALU.mult, ALU.add).then_inc(bias_ready, 1)

            for u in range(6):
                unit(u, u % 2, True)
            with dve.Fori(3, UNITS // 2) as i:
                for j in range(2):
                    unit(2 * i + j, j, False)
            for w_ in range(UNITS - LAG_PV - 1, UNITS):
                take_o(w_)


def ffn(nc, io, keep):
    x, ident, sv, o, sums = keep["x"], keep["ident"], keep["sv"], keep["o"], keep["sums"]
    with ExitStack() as ctx:
        def sb(name, shape, dt=F32):
            return ctx.enter_context(nc.sbuf_tensor(name, shape, dt))

        def psum(name, shape, dt=F32):
            return ctx.enter_context(nc.psum_tensor(name, shape, dt))

        def sem(name):
            return ctx.enter_context(nc.semaphore(name))

        wp = sb("wp", [P, KD, D])
        bp = sb("bp", [P, D])
        gates = sb("gates", [P, 2])
        tgates = sb("tgates", [P, 2])
        rsum = sb("rsum", [P, UNITS])
        on = sb("on", [P, QT, D])
        xT = sb("xT", [P, KD, NQ])
        y = sb("y", [P, QT, D])
        stats = sb("stats2", [P, QT, 6])
        mv = sb("mv2", [P, QT, 2])
        ln = sb("ln2", [P, 4, QT])
        router = sb("router", [P, KD, E + 1])
        lmax = sb("lmax", [P, QT])
        probs = sb("probs", [P, QT, E])
        psums = sb("psums", [P, QT])
        top = sb("top", [P, QT, TOPK])
        rest = sb("rest", [P, QT, E])
        sig = sb("sig", [P, QT])
        share = sb("share", [P, QT, E + 1])
        wgu = sb("wgu", [P, 2, KD, 2 * EG * I])
        wdn = sb("wdn", [P, 2, 2, D])
        th = sb("th", [P, 2, EG * I])
        gl = sb("gl", [P, 2, EG * I])
        gu = sb("gu", [P, 2, EG * I])
        act_in = sb("act_in", [P, 2, EG * I])
        aT = sb("aT", [P, 2, 2 * P])

        pacc = psum("pacc", [P, QT, D])
        pgu = psum("pgu", [P, 2, 2 * EG * I])
        pat = psum("pat", [P, 2, KC])
        wide = pacc[:, :, :].rearrange("p t d -> p (t d)")

        loaded = sem("loaded3")
        tanhs = sem("tanhs")
        steps = sem("steps3")
        o_ready = sem("o_ready")
        turned = sem("turned3")
        xT_ready = sem("xT_ready")
        root = sem("root3")
        proj = sem("proj")
        h_ready = sem("h_ready3")
        routed = sem("routed")
        shifted = sem("shifted")
        exped = sem("exped3")
        share_ready = sem("share_ready")
        gu_in = [sem("gu_in0"), sem("gu_in1")]
        dn_in = [sem("dn_in0"), sem("dn_in1")]
        gu_ready = sem("gu_ready")
        th_ready = sem("th_ready")
        gl_ready = sem("gl_ready")
        gu_done = sem("gu_done")
        a_ready = sem("a_ready")
        a_turned = sem("a_turned")
        aT_ready = sem("aT_ready")
        added = sem("added")
        y_ready = sem("y_ready")
        out_done = sem("out_done")

        block = ctx.enter_context(nc.Block())
        NU = (NEG + 1) * QT
        LAG_T, LAG_D = 2, 3

        @block.sync
        def _(sp):
            for dst, src in ((wp[:, :, :], io["Wp"].rearrange("(k p) n -> p k n", p=P)),
                             (bp[:, :], io["bp"].broadcast_to([P, D])),
                             (gates[:, 0:1], io["g_xattn"].broadcast_to([P, 1])),
                             (gates[:, 1:2], io["g_ffn"].broadcast_to([P, 1])),
                             (router[:, :, :], io["router"].rearrange("(k p) n -> p k n", p=P))):
                sp.dma_start(dst, src).then_inc(loaded, 16)

            def load_gu(g, par):
                sp.dma_start(wgu[:, par], io["gate_up"][bass.ds(g, 1)].rearrange("o (k p) n -> p (o k) n", p=P))\
                  .then_inc(gu_in[par], 16)

            def load_dn(g, par):
                sp.dma_start(wdn[:, par], io["down"][bass.ds(g, 1)].rearrange("o (k p) n -> p (o k) n", p=P))\
                  .then_inc(dn_in[par], 16)

            for g in range(2):
                load_gu(g, g)
                load_dn(g, g)
            with sp.Fori(1, NEG // 2) as i:
                for par in range(2):
                    g = 2 * i + par
                    sp.wait_ge(gu_ready, QT * (g - 1))
                    load_gu(g, par)
                    sp.wait_ge(added, QT * (g - 1))
                    load_dn(g, par)
            sp.wait_ge(gu_ready, QT * (NEG - 1))
            sp.dma_start(wgu[:, 0, :, 0:2 * I], io["shared_gate_up"].rearrange("(k p) n -> p k n", p=P)).then_inc(gu_in[0], 16)
            sp.wait_ge(added, QT * (NEG - 1))
            sp.dma_start(wdn[0:I, 0, 0, :], io["shared_down"]).then_inc(dn_in[0], 16)
            out = io["out"].rearrange("(t p) d -> p t d", p=P)
            for half in range(2):
                sp.wait_ge(y_ready, half + 1)
                sp.dma_start(out[:, 4 * half:4 * half + 4, :], y[:, 4 * half:4 * half + 4, :]).then_inc(out_done, 16)
            sp.wait_ge(out_done, 32)

        @block.tensor
        def _(pe):
            def turn_rows(src):
                for k in range(KD):
                    for t in range(QT):
                        mm = nc.tensor.transpose(wide[:, k * NQ + t * P:k * NQ + (t + 1) * P],
                                                 src[:, t, k * P:(k + 1) * P], ident[:, :])
                    mm.then_inc(turned, 1)

            pe.wait_ge(loaded, 16 * 5)
            pe.wait_ge(o_ready, 1)
            turn_rows(on)
            pe.wait_ge(xT_ready, 2)
            for t in range(QT):
                for k in range(KD):
                    mm = nc.tensor.matmul(pacc[:, t, :], xT[:, k, t * P:(t + 1) * P], wp[:, k, :],
                                          start=(k == 0), stop=(k == KD - 1))
            mm.then_inc(proj, 1)
            pe.wait_ge(h_ready, 1)
            turn_rows(on)
            pe.wait_ge(xT_ready, 4)
            for t in range(QT):
                for k in range(KD):
                    mm = nc.tensor.matmul(pat[:, t // 4, (t % 4) * P:(t % 4) * P + E + 1],
                                          xT[:, k, t * P:(t + 1) * P], router[:, k, :],
                                          start=(k == 0), stop=(k == KD - 1))
            mm.then_inc(routed, 1)

            def gate_up(n, g_par, t, loads, early, width=2 * EG * I):
                if t == 0:
                    pe.wait_ge(gu_in[g_par], 16 * loads)
                if not (early and n < 2):
                    pe.wait_ge(gu_done, n - 1)
                for k in range(KD):
                    mm = nc.tensor.matmul(pgu[:, t % 2, 0:width], xT[:, k, t * P:(t + 1) * P],
                                          wgu[:, g_par, k, 0:width], start=(k == 0), stop=(k == KD - 1))
                mm.then_inc(gu_ready, 1)

            def turn(n, b, early, width=EG * I):
                pe.wait_ge(a_ready, n + 1)
                if not (early and n < 2):
                    pe.wait_ge(aT_ready, n - 1)
                for k in range(-(-width // P)):
                    m = min(P, width - k * P)
                    mm = nc.tensor.transpose(pat[0:m, b, k * P:(k + 1) * P], act_in[:, b, k * P:k * P + m], ident[:, :])
                mm.then_inc(a_turned, 1)

            def add(n, b, t, g_par, loads, width=EG * I):
                if t == 0:
                    pe.wait_ge(dn_in[g_par], 16 * loads)
                pe.wait_ge(aT_ready, n + 1)
                for k in range(-(-width // P)):
                    m = min(P, width - k * P)
                    mm = nc.tensor.matmul(pacc[:, t, :], aT[0:m, b, k * P:(k + 1) * P], wdn[0:m, g_par, k, :],
                                          start=False, stop=False, skip_group_check=True)
                mm.then_inc(added, 1)

            pe.wait_ge(share_ready, 1)
            def group(base, i, g_par, early, last=False):
                for t in range(QT):
                    n = base + t
                    gate_up(n, g_par, t, i + 1, early, 2 * I if last else 2 * EG * I)
                    tb, db = (t - LAG_T) % QT, (t - LAG_D) % QT
                    if not (early and n < LAG_T):
                        turn(n - LAG_T, t % 2, early, I if last and t >= LAG_T else EG * I)
                    if not (early and n < LAG_D):
                        same = t >= LAG_D
                        dl = (i + 1) if same or g_par == 1 else i
                        add(n - LAG_D, (t - LAG_D) % 2, db, g_par if same else 1 - g_par, dl,
                            I if last and same else EG * I)

            group(0, 0, 0, True)
            group(QT, 0, 1, False)
            with pe.Fori(1, NEG // 2) as i:
                for par in range(2):
                    group(2 * QT * i + QT * par, i, par, False)
            group(NEG * QT, NEG // 2, 0, False, last=True)
            for t in range(LAG_D):
                n = NU + t
                if t < LAG_T:
                    turn(n - LAG_T, t % 2, False, I)
                add(n - LAG_D, (n - LAG_D) % 2, QT - LAG_D + t, 0, NEG // 2 + 1, I)

        @block.scalar
        def _(act):
            act.wait_ge(loaded, 16 * 5)
            nc.scalar.activation(tgates[:, :], gates[:, :], ACT.Tanh).then_inc(tanhs, 1)

            def take_rows(n):
                for k in range(KD):
                    act.wait_ge(turned, n + k + 1)
                    nc.scalar.copy(xT[:, k, :], wide[:, k * NQ:(k + 1) * NQ]).then_inc(xT_ready, 1)

            take_rows(0)
            act.wait_ge(steps, BEFORE_LN + VAR_STEP)
            nc.scalar.activation(ln[:, 1, :], ln[:, 0, :], ACT.Sqrt).then_inc(root, 1)
            take_rows(2)
            act.wait_ge(shifted, 1)
            nc.scalar.activation(probs[:, :, :], probs[:, :, :], ACT.Exp).then_inc(exped, 1)
            nc.scalar.activation(sig[:, :], sig[:, :], ACT.Tanh, scale=0.5).then_inc(exped, 1)

            def tanh(n, b, early, width=EG * I):
                act.wait_ge(gu_ready, n + 1)
                if not (early and n < 2):
                    act.wait_ge(gl_ready, n - 1)
                nc.scalar.activation(th[:, b, 0:width], pgu[:, b, 0:width], ACT.Tanh, scale=0.5).then_inc(th_ready, 1)

            def take(n, b, early, width=EG * I):
                act.wait_ge(a_turned, n + 1)
                if not (early and n < 2):
                    act.wait_ge(added, n - 1)
                m, w = (P, width) if width > P else (width, P)
                nc.scalar.copy(aT[0:m, b, 0:w], pat[0:m, b, 0:w]).then_inc(aT_ready, 1)

            tanh(0, 0, True)
            tanh(1, 1, True)
            for n in range(2, 4):
                tanh(n, n % 2, False)
                take(n - 2, n % 2, True)
            with act.Fori(2, NEG * QT // 2) as i:
                for b in range(2):
                    tanh(2 * i + b, b, False)
                    take(2 * i + b - 2, b, False)
            for n in range(NEG * QT, NU + 2):
                if n < NU:
                    tanh(n, n % 2, False, I)
                take(n - 2, n % 2, False, I if n - 2 >= NEG * QT else EG * I)

        @block.gpsimd
        def _(pool):
            def weigh(n, b, t, col, early, experts=EG):
                pool.wait_ge(gu_done, n + 1)
                if not (early and n < 2):
                    pool.wait_ge(a_turned, n - 1)
                w = experts * I
                nc.gpsimd.tensor_tensor(act_in[:, b, 0:w].rearrange("p (e i) -> p e i", e=experts),
                                        gu[:, b, 0:w].rearrange("p (e i) -> p e i", e=experts),
                                        last_axis(share[:, t, bass.ds(col, experts)], I), ALU.mult).then_inc(a_ready, 1)

            pool.wait_ge(share_ready, 1)
            for t in range(QT):
                weigh(t, t % 2, t, 0, True)
            with pool.Fori(1, NEG) as g:
                for t in range(QT):
                    weigh(QT * g + t, t % 2, t, EG * g, False)
            for t in range(QT):
                weigh(NEG * QT + t, t % 2, t, E, False, 1)

        @block.vector
        def _(dve):
            c = Steps(dve, steps)
            dve.wait_ge(loaded, 16 * 5)
            c.then(nc.vector.reciprocal(rsum[:, :], sums[:, :]))
            c.then(nc.vector.tensor_tensor(o[:, :].rearrange("p (u d) -> p u d", d=HD),
                                           o[:, :].rearrange("p (u d) -> p u d", d=HD),
                                           last_axis(rsum[:, :], HD), ALU.mult))
            ov = o[:, :].rearrange("p (g h j d) -> p g j h d", h=H, j=2, d=HD)
            for t in range(QT):
                done = nc.vector.tensor_tensor(on[:, t, :].rearrange("p (h d) -> p h d", h=H), ov[:, t // 2, t % 2],
                                               sv[:, :].rearrange("p (h d) -> p h d", h=H), ALU.mult)
            done.then_inc(o_ready, 1)
            dve.wait_ge(proj, 1)
            dve.wait_ge(tanhs, 1)
            c.then(nc.vector.tensor_tensor(y[:, :, :], pacc[:, :, :], middle_axis(bp[:, :], QT), ALU.add))
            c.then(nc.vector.scalar_tensor_tensor(x[:, :, :], y[:, :, :], tgates[:, 0:1], x[:, :, :], ALU.mult, ALU.add))
            assert c.n == BEFORE_LN
            layernorm(nc, dve, Steps(dve, steps, BEFORE_LN), x, stats, mv, ln, on, root, h_ready)
            c.n += LN_STEPS

            dve.wait_ge(routed, 1)
            logits = pat[:, :, :].rearrange("p b (t n) -> p (b t) n", n=P)
            c.then(nc.vector.tensor_reduce(lmax[:, :], logits[:, :, 0:E], AX.X, ALU.max))
            nc.vector.tensor_copy(sig[:, :], logits[:, :, E])
            nc.vector.tensor_tensor(probs[:, :, :], logits[:, :, 0:E], last_axis(lmax[:, :], E),
                                    ALU.subtract).then_inc(shifted, 1)
            nc.vector.memset(pacc[:, :, :], 0.0)
            dve.wait_ge(exped, 2)
            c.then(nc.vector.tensor_reduce(psums[:, :], probs[:, :, :], AX.X, ALU.add))
            c.then(nc.vector.reciprocal(psums[:, :], psums[:, :]))
            c.then(nc.vector.tensor_tensor(probs[:, :, :], probs[:, :, :], last_axis(psums[:, :], E), ALU.mult))
            for t in range(QT):
                done = nc.vector.max(top[:, t, :], probs[:, t, :])
            c.then(done)
            for t in range(QT):
                done = nc.vector.match_replace(rest[:, t, :], top[:, t, :], probs[:, t, :], -1.0)
            c.then(done)
            c.then(nc.vector.tensor_reduce(lmax[:, :], top[:, :, :], AX.X, ALU.add))
            c.then(nc.vector.reciprocal(lmax[:, :], lmax[:, :]))
            c.then(nc.vector.tensor_scalar(lmax[:, :], lmax[:, :], 0.5, None, ALU.mult))
            c.then(nc.vector.scalar_tensor_tensor(probs[:, :, :], rest[:, :, :], 0.0, probs[:, :, :], ALU.is_lt, ALU.mult))
            nc.vector.tensor_tensor(share[:, :, 0:E], probs[:, :, :], last_axis(lmax[:, :], E), ALU.mult)
            nc.vector.tensor_scalar(share[:, :, E], sig[:, :], 1.0, 0.25, ALU.add, ALU.mult).then_inc(share_ready, 1)

            def times(n, b, early, width=EG * I):
                dve.wait_ge(th_ready, n + 1)
                if not (early and n < 1):
                    dve.wait_ge(gu_done, n)
                nc.vector.scalar_tensor_tensor(gl[:, b, 0:width], th[:, b, 0:width], 1.0, pgu[:, b, 0:width],
                                               ALU.add, ALU.mult).then_inc(gl_ready, 1)
                dve.wait_ge(gl_ready, n + 1)
                if not (early and n < 2):
                    dve.wait_ge(a_ready, n - 1)
                nc.vector.tensor_tensor(gu[:, b, 0:width], gl[:, b, 0:width], pgu[:, b, width:2 * width],
                                        ALU.mult).then_inc(gu_done, 1)

            times(0, 0, True)
            times(1, 1, True)
            with dve.Fori(1, NEG * QT // 2) as i:
                for b in range(2):
                    times(2 * i + b, b, False)
            for n in range(NEG * QT, NU):
                times(n, n % 2, False, I)
            dve.wait_ge(added, NU)
            for half in range(2):
                ts = slice(4 * half, 4 * half + 4)
                nc.vector.scalar_tensor_tensor(y[:, ts, :], pacc[:, ts, :], tgates[:, 1:2], x[:, ts, :],
                                               ALU.mult, ALU.add).then_inc(y_ready, 1)


def program(nc, io):
    with ExitStack() as ctx:
        def sb(name, shape, dt=F32):
            return ctx.enter_context(nc.sbuf_tensor(name, shape, dt))

        keep = {
            "x": sb("x", [P, QT, D]),
            "ident": sb("ident", [P, P]),
            "sq": sb("sq", [P, STEPS, 2]),
            "sv": sb("sv", [P, D]),
            "o": sb("o", [P, UNITS * HD]),
            "sums": sb("sums", [P, UNITS]),
        }
        scratch = (nc.dram_tensor("kT_parts", (H, QR, NK), BF16, kind="Internal").ap(),
                   nc.dram_tensor("qT_parts", (H, QR, NQ), BF16, kind="Internal").ap(),
                   nc.dram_tensor("v_ints", (H, P, VT * HD), BF16, kind="Internal").ap())
        projections(nc, io, keep, scratch)
        attention(nc, keep, scratch)
        ffn(nc, io, keep)


def kernel(**inputs):
    import numpy as np
    import concourse.bacc as bacc
    from concourse.bass_utils import run_bass_kernel_spmd

    g = {k: np.asarray(a) for k, a in inputs.items()}
    gu = g["L0_ffn_gate_up_proj"].reshape(NEG, EG, 2, I, D)
    arrays = {
        "x": g["x"].reshape(NQ, D),
        "ctxT": g["ctx_2048"].reshape(NK, D).T,
        "eye": np.eye(P, dtype=np.float32),
        "Wq": g["L0_xattn_Wq"], "bq": g["L0_xattn_bq"].reshape(1, D),
        "Wkv": g["L0_xattn_Wkv"], "bkv": g["L0_xattn_bkv"].reshape(1, 2 * D),
        "Wp": g["L0_xattn_Wp"], "bp": g["L0_xattn_bp"].reshape(1, D),
        "g_xattn": g["g_xattn"].reshape(1, 1), "g_ffn": g["g_ffn"].reshape(1, 1),
        "router": np.concatenate([g["L0_ffn_router_w"], g["L0_ffn_shared_expert_gate_w"]], 0).T,
        "gate_up": gu.transpose(0, 4, 2, 1, 3).reshape(NEG, D, 2 * EG * I),
        "down": g["L0_ffn_down_proj"].transpose(0, 2, 1).reshape(NEG, EG * I, D),
        "shared_gate_up": np.concatenate([g["L0_ffn_shared_gate_w"], g["L0_ffn_shared_up_w"]], 0).T,
        "shared_down": g["L0_ffn_shared_down_w"].T,
    }
    nc = bacc.Bacc("TRN2", target_bir_lowering=False, num_devices=1)
    io, feed = {}, {}
    for name, a in arrays.items():
        feed[f"in_{name}"] = np.ascontiguousarray(a)
        io[name] = nc.dram_tensor(f"in_{name}", a.shape, mybir.dt.from_np(a.dtype), kind="ExternalInput").ap()
    io["out"] = nc.dram_tensor("out_x", (NQ, D), F32, kind="ExternalOutput").ap()
    program(nc, io)
    r = run_bass_kernel_spmd(nc, [feed], core_ids=[0])
    return r.results[0]["out_x"].reshape(4, NQ // 4, D)
```

```python
from contextlib import ExitStack

import concourse.bass as bass
from concourse import mybir

F32 = mybir.dt.float32
F32R = mybir.dt.float32r
BF16 = mybir.dt.bfloat16
U8 = mybir.dt.uint8
U32 = mybir.dt.uint32
ALU = mybir.AluOpType
ACT = mybir.ActivationFunctionType
AX = mybir.AxisListType

P = 128
D = 256
KD = D // P
H = 16
HD = D // H
NQ = 1024
QT = NQ // P
NK = 6404
KC = 512
NKC = NK // KC
TAIL = NK - NKC * KC
TAILW = TAIL // 4
VT = 4 * (NKC + 1)
PARTS = 3
QR = PARTS * HD
HP = 64
SC = 1024
SCS = [(a, min(SC, NK - a)) for a in range(0, NK, SC)]
NSC = len(SCS)
UNITS = H * QT
STEPS = UNITS // 2
WG = 4
E = 64
I = 64
EG = 4
NEG = E // EG
TOPK = 8
RW = E + 2
ROUND = 1.5 * 2.0 ** 23
LN255 = 5.541263545158426
LN_EPS = 1e-5
QMIN = 1e-8


def last_axis(ap, n):
    return ap.unsqueeze(len(ap.shape)).broadcast_to(list(ap.shape) + [n])


def middle_axis(ap, n):
    return ap.unsqueeze(1).broadcast_to([ap.shape[0], n, ap.shape[1]])


def product(nc, out, stationary, moving, start, stop, **kw):
    (a_hi, a_lo), (b_hi, b_lo) = stationary, moving
    nc.tensor.matmul(out, a_hi, b_hi, start=start, stop=False, **kw)
    nc.tensor.matmul(out, a_hi, b_lo, start=False, stop=False, **kw)
    return nc.tensor.matmul(out, a_lo, b_hi, start=False, stop=stop, **kw)


class Steps:

    def __init__(self, engine, sem, base=0):
        self.engine, self.sem, self.n, self.base = engine, sem, 0, base

    def then(self, instruction):
        instruction.then_inc(self.sem, 1)
        self.n += 1
        self.engine.wait_ge(self.sem, self.base + self.n)


LN_STEPS = 8
BEFORE_LN = 4
VAR_STEP = 3


def layernorm(nc, dve, steps, x, stats, mv, ln, out, root, ready):
    for t in range(QT):
        done = nc.vector.bn_stats(stats[:, t, :], x[:, t, :])
    steps.then(done)
    for t in range(QT):
        done = nc.vector.bn_aggr(mv[:, t, :], stats[:, t, :])
    steps.then(done)
    steps.then(nc.vector.tensor_scalar(ln[:, 0, :], mv[:, :, 1], LN_EPS, None, ALU.add))
    assert steps.n == VAR_STEP
    dve.wait_ge(root, 1)
    steps.then(nc.vector.reciprocal(ln[:, 2, :], ln[:, 1, :]))
    steps.then(nc.vector.tensor_tensor(ln[:, 3, :], ln[:, 0, :], ln[:, 2, :], ALU.mult))
    steps.then(nc.vector.tensor_tensor(ln[:, 3, :], ln[:, 3, :], ln[:, 2, :], ALU.mult))
    steps.then(nc.vector.tensor_scalar(ln[:, 3, :], ln[:, 3, :], -0.5, 1.5, ALU.mult, ALU.add))
    steps.then(nc.vector.tensor_tensor(ln[:, 2, :], ln[:, 2, :], ln[:, 3, :], ALU.mult))
    for t in range(QT):
        done = nc.vector.tensor_scalar(out[:, t, :], x[:, t, :], mv[:, t, 0:1], ln[:, 2, t:t + 1],
                                       ALU.subtract, ALU.mult)
    done.then_inc(ready, 1)
    dve.wait_ge(ready, 1)
    assert steps.n == LN_STEPS


def projections(nc, io, keep, scratch):
    x, ident, sv = keep["x"], keep["ident"], keep["sv"]
    sq = keep["sq"]
    kT_d, qT_d, v_d = scratch
    with ExitStack() as ctx:
        def sb(name, shape, dt=F32):
            return ctx.enter_context(nc.sbuf_tensor(name, shape, dt))

        def psum(name, shape, dt=F32):
            return ctx.enter_context(nc.psum_tensor(name, shape, dt))

        def sem(name):
            return ctx.enter_context(nc.semaphore(name))

        identb = sb("identb", [P, P], BF16)
        ones = sb("ones", [P, P])
        wq = sb("wq", [P, KD, D])
        wkv = sb("wkv", [P, KD, 2 * D])
        bq = sb("bq", [P, D])
        bkv = sb("bkv", [P, 2 * D])
        stats = sb("stats", [P, QT, 6])
        mv = sb("mv", [P, QT, 2])
        ln = sb("ln", [P, 4, QT])
        h = sb("h", [P, QT, D])
        hT = sb("hT", [P, KD, NQ])
        ctxc = sb("ctxc", [P, 2, KD, KC])
        kf = sb("kf", [P, 4, D])
        kr = sb("kr", [P, 4, D])
        kq = sb("kq", [P, 2, 4, D])
        kres = sb("kres", [P, 4, D])
        amax = sb("amax", [P, 4 * H])
        kscale = sb("kscale", [P, 4 * H])
        kinv = sb("kinv", [P, 4 * H])
        parts = sb("parts", [P, 2, 4, H, HP], BF16)
        turned = sb("turned", [P, 2, H // 2, KC], BF16)
        vf = sb("vf", [P, VT, D])
        vmax = sb("vmax", [P, D])
        vcol = sb("vcol", [P, KD])
        vdiag = sb("vdiag", [P, KD, P])
        vinv = sb("vinv", [P, D])
        vr = sb("vr", [P, VT, 4 * HD])
        vint = sb("vint", [P, 2, 4, VT, HD], BF16)

        pk = psum("pk", [P, 4, D])
        pv = psum("pv", [P, 4, D])
        pt = psum("pt", [P, H // 2, KC], BF16)
        ptf = pt[:, :, :].rearrange("p a b -> p (a b)").bitcast(F32)

        loaded = sem("loaded")
        ctx_in = [sem("ctx_in0"), sem("ctx_in1")]
        consts = sem("consts")
        qsteps = sem("qsteps")
        root = sem("root")
        h_ready = sem("h_ready")
        hT_turned = sem("hT_turned")
        hT_ready = sem("hT_ready")
        q_ready = sem("q_ready")
        q_taken = sem("q_taken")
        qparts = sem("qparts")
        k_ready = sem("k_ready")
        v_ready = sem("v_ready")
        ksteps = sem("ksteps")
        k_taken = sem("k_taken")
        kq_ready = sem("kq_ready")
        v_taken = sem("v_taken")
        hi_done = sem("hi_done")
        res_done = sem("res_done")
        mid_done = sem("mid_done")
        kparts = sem("kparts")
        turned_ready = sem("turned_ready")
        turned_taken = sem("turned_taken")
        stored = [sem("stored0"), sem("stored1")]
        vsteps = sem("vsteps")
        v_turned = sem("v_turned")
        v_diag = sem("v_diag")
        v_bcast = sem("v_bcast")
        vint_ready = sem("vint_ready")
        v_stored = [sem("v_stored0"), sem("v_stored1")]

        block = ctx.enter_context(nc.Block())
        LK = 5
        ctx_view = io["ctxT"].rearrange("(k p) n -> p k n", p=P)

        @block.sync
        def _(sp):
            for dst, src in ((x[:, :, :], io["x"].rearrange("(t p) d -> p t d", p=P)),
                             (ident[:, :], io["eye"]),
                             (bq[:, :], io["bq"].broadcast_to([P, D])),
                             (bkv[:, :], io["bkv"].broadcast_to([P, 2 * D])),
                             (wq[:, :, :], io["Wq"].rearrange("(k p) n -> p k n", p=P)),
                             (wkv[:, :, :], io["Wkv"].rearrange("(k p) n -> p k n", p=P))):
                sp.dma_start(dst, src).then_inc(loaded, 16)

            def load(c, par, width):
                sp.dma_start(ctxc[:, par, :, 0:width],
                             ctx_view[:, :, bass.ds(c * KC, width)]).then_inc(ctx_in[par], 16)

            def store(n, par, dram, at, width):
                sp.wait_ge(turned_taken, n + 1)
                for half in range(2):
                    dst = dram.rearrange("(g two) r n -> two r g n", two=2)[half]
                    sp.dma_start(dst[:, :, bass.ds(at, width)],
                                 turned[HP * half:HP * half + QR, par, :, 0:width]).then_inc(stored[par], 16)

            load(0, 0, KC)
            load(1, 1, KC)
            for r in range(2):
                store(r, r, qT_d, r * KC, KC)
            with sp.Fori(0, NKC // 2 - 1) as i:
                for par in range(2):
                    c = 2 * i + par
                    sp.wait_ge(v_ready, c + 1)
                    load(c + 2, par, KC)
                    store(c + 2, par, kT_d, c * KC, KC)
            sp.wait_ge(v_ready, NKC - 1)
            load(NKC, 0, TAIL)
            store(NKC, 0, kT_d, (NKC - 2) * KC, KC)
            store(NKC + 1, 1, kT_d, (NKC - 1) * KC, KC)
            store(NKC + 2, 0, kT_d, NKC * KC, TAIL)
            for n in range(4):
                sp.wait_ge(vint_ready, n + 1)
                sp.dma_start(v_d.rearrange("h p n -> p h n")[:, 4 * n:4 * n + 4, :],
                             vint[:, n % 2].rearrange("p h t d -> p h (t d)")).then_inc(v_stored[n % 2], 16)
            sp.wait_ge(stored[0], 32 * (NKC // 2 + 2))
            sp.wait_ge(stored[1], 32 * (NKC // 2 + 1))
            for b in range(2):
                sp.wait_ge(v_stored[b], 32)

        @block.gpsimd
        def _(pool):
            pool.memset(ones[:, :], 1.0).then_inc(consts, 1)
            pool.memset(parts[:, :, :, :, :].rearrange("p a b h n -> p (a b h n)").bitcast(U32), 0).then_inc(consts, 1)
            pool.memset(vf[:, VT - 4:VT, :], 0.0).then_inc(consts, 1)

            def residuals(c, par):
                pool.wait_ge(hi_done, c + 1)
                if not (isinstance(c, int) and c == 0):
                    pool.wait_ge(kparts, c)
                pool.tensor_tensor(kres[:, :, :].rearrange("p i (h e) -> p i h e", h=H),
                                   kq[:, par].rearrange("p i (h e) -> p i h e", h=H),
                                   parts[:, par, :, :, 0:HD], ALU.subtract).then_inc(res_done, 1)
                pool.wait_ge(mid_done, c + 1)
                pool.tensor_tensor(parts[:, par, :, :, 2 * HD:3 * HD],
                                   kres[:, :, :].rearrange("p i (h e) -> p i h e", h=H),
                                   parts[:, par, :, :, HD:2 * HD], ALU.subtract).then_inc(kparts, 1)

            residuals(0, 0)
            residuals(1, 1)
            with pool.Fori(1, NKC // 2) as i:
                for par in range(2):
                    residuals(2 * i + par, par)
            residuals(NKC, 0)

        @block.scalar
        def _(act):
            act.wait_ge(qsteps, VAR_STEP)
            nc.scalar.activation(ln[:, 1, :], ln[:, 0, :], ACT.Sqrt).then_inc(root, 1)
            for k in range(KD):
                act.wait_ge(hT_turned, k + 1)
                nc.scalar.copy(hT[:, k, :], ptf[:, k * NQ:(k + 1) * NQ]).then_inc(hT_ready, 1)

            def first_parts(c, par):
                act.wait_ge(kq_ready, c + 1)
                act.wait_ge(turned_ready, c + 1)
                nc.scalar.copy(parts[:, par, :, :, 0:HD],
                               kq[:, par].rearrange("p i (h e) -> p i h e", h=H)).then_inc(hi_done, 1)

            def second_parts(c, par):
                act.wait_ge(res_done, c + 1)
                nc.scalar.copy(parts[:, par, :, :, HD:2 * HD],
                               kres[:, :, :].rearrange("p i (h e) -> p i h e", h=H)).then_inc(mid_done, 1)

            def evacuate_item(n, par, uses):
                act.wait_ge(turned_ready, n + 1)
                if not (isinstance(uses, int) and uses == 0):
                    act.wait_ge(stored[par], 32 * uses)
                nc.scalar.copy(turned[:, par, :, :], pt[:, :, :]).then_inc(turned_taken, 1)

            evacuate_item(0, 0, 0)
            first_parts(0, 0)
            evacuate_item(1, 1, 0)
            second_parts(0, 0)
            first_parts(1, 1)
            evacuate_item(2, 0, 1)
            second_parts(1, 1)
            with act.Fori(1, NKC // 2) as i:
                first_parts(2 * i, 0)
                evacuate_item(2 * i + 1, 1, i)
                second_parts(2 * i, 0)
                first_parts(2 * i + 1, 1)
                evacuate_item(2 * i + 2, 0, i + 1)
                second_parts(2 * i + 1, 1)
            first_parts(NKC, 0)
            evacuate_item(NKC + 1, 1, NKC // 2)
            second_parts(NKC, 0)
            evacuate_item(NKC + 2, 0, NKC // 2 + 1)

        @block.tensor
        def _(pe):
            pe.wait_ge(h_ready, 1)
            for k in range(KD):
                for t in range(QT):
                    mm = nc.tensor.transpose(ptf[:, k * NQ + t * P:k * NQ + (t + 1) * P],
                                             h[:, t, k * P:(k + 1) * P], ident[:, :])
                mm.then_inc(hT_turned, 1)
            pe.wait_ge(hT_ready, KD)
            for t in range(QT):
                out = (pk if t < 4 else pv)[:, t % 4, :]
                for k in range(KD):
                    mm = nc.tensor.matmul(out, hT[:, k, t * P:(t + 1) * P], wq[:, k, :],
                                          start=(k == 0), stop=(k == KD - 1))
            mm.then_inc(q_ready, 1)

            def turn(n, par):
                if not (isinstance(n, int) and n == 0):
                    pe.wait_ge(turned_taken, n)
                for i in range(4):
                    for g in range(H // 2):
                        mm = nc.tensor.transpose(
                            pt[:, g, i * P:(i + 1) * P],
                            parts[:, par, i, 2 * g:2 * g + 2, :].rearrange("p a b -> p (a b)"), identb[:, :])
                mm.then_inc(turned_ready, 1)

            def project(c, par, width, loads):
                pe.wait_ge(ctx_in[par], 16 * loads)
                if isinstance(c, int) and c == 0:
                    pe.wait_ge(q_taken, 2)
                else:
                    pe.wait_ge(k_taken, c)
                for i in range(-(-width // P)):
                    m = min(P, width - i * P)
                    for k in range(KD):
                        mm = nc.tensor.matmul(pk[0:m, i, :], ctxc[:, par, k, i * P:i * P + m], wkv[:, k, 0:D],
                                              start=(k == 0), stop=(k == KD - 1))
                mm.then_inc(k_ready, 1)
                if not (isinstance(c, int) and c == 0):
                    pe.wait_ge(v_taken, c)
                for b in range(4):
                    for k in range(KD):
                        mm = nc.tensor.matmul(pv[0:width // 4, b, :], ctxc[:, par, k, b:width:4], wkv[:, k, D:2 * D],
                                              start=(k == 0), stop=(k == KD - 1))
                mm.then_inc(v_ready, 1)

            project(0, 0, KC, 1)
            for r in range(2):
                pe.wait_ge(qparts, r + 1)
                turn(r, r)
            project(1, 1, KC, 1)
            pe.wait_ge(kparts, 1)
            turn(2, 0)
            with pe.Fori(1, NKC // 2) as i:
                for par in range(2):
                    project(2 * i + par, par, KC, i + 1)
                    pe.wait_ge(kparts, 2 * i + par)
                    turn(2 * i + par + 1, 1 - par)
            project(NKC, 0, TAIL, NKC // 2 + 1)
            for c in (NKC - 1, NKC):
                pe.wait_ge(kparts, c + 1)
                turn(c + 2, c % 2)

            pe.wait_ge(vsteps, 1)
            for k in range(KD):
                mm = nc.tensor.transpose(pk[:, 0, k * P:(k + 1) * P], vmax[:, k * P:(k + 1) * P], ident[:, :])
            mm.then_inc(v_turned, 1)
            pe.wait_ge(v_diag, 1)
            mm = nc.tensor.matmul(pk[:, 2, :], ones[:, :], vdiag[:, :, :].rearrange("p k n -> p (k n)"),
                                  start=True, stop=True)
            mm.then_inc(v_bcast, 1)

        @block.vector
        def _(dve):
            q = Steps(dve, qsteps)
            dve.wait_ge(loaded, 16 * 6)
            dve.wait_ge(consts, 3)
            nc.vector.tensor_copy(identb[:, :], ident[:, :])
            layernorm(nc, dve, q, x, stats, mv, ln, h, root, h_ready)
            dve.wait_ge(q_ready, 1)
            for r, bank in enumerate((pk, pv)):
                nc.vector.tensor_tensor(kf[:, :, :], bank[:, :, :], middle_axis(bq[:, :], 4),
                                        ALU.add).then_inc(q_taken, 1)
                dve.wait_ge(q_taken, r + 1)
                q.then(nc.vector.tensor_reduce(amax[:, :], kf[:, :, :].rearrange("p i (h e) -> p (i h) e", e=HD),
                                               AX.X, ALU.max, apply_absolute_value=True))
                q.then(nc.vector.tensor_scalar(kscale[:, :], amax[:, :], 1.0 / 127.0, 4 * QMIN, ALU.mult, ALU.max))
                q.then(nc.vector.reciprocal(kinv[:, :], kscale[:, :]))
                nc.vector.tensor_scalar(
                    sq[:, 2 * r * H:2 * (r + 1) * H, :].rearrange("p (g h) j -> p g h j", h=H),
                    kscale[:, :].rearrange("p (g j h) -> p g h j", g=2, j=2), 0.25, None, ALU.mult)
                q.then(nc.vector.tensor_tensor(kr[:, :, :].rearrange("p i (h e) -> p (i h) e", e=HD),
                                               kf[:, :, :].rearrange("p i (h e) -> p (i h) e", e=HD),
                                               last_axis(kinv[:, :], HD), ALU.mult))
                for part in range(PARTS):
                    done = nc.vector.tensor_scalar(
                        parts[:, r, :, :, part * HD:(part + 1) * HD].rearrange("p i h e -> p (i h) e"),
                        kr[:, :, :].rearrange("p i (h e) -> p (i h) e", e=HD), ROUND, ROUND, ALU.add, ALU.subtract)
                done.then_inc(qparts, 1)
                dve.wait_ge(qparts, r + 1)

            def quantise(c, par, rows):
                k = Steps(dve, ksteps, LK * c)
                dve.wait_ge(k_ready, c + 1)
                heads = lambda t: t.rearrange("p i (h e) -> p (i h) e", e=HD)
                nc.vector.tensor_tensor(kf[:, :, :], pk[:, :, :], middle_axis(bkv[:, 0:D], 4),
                                        ALU.add).then_inc(k_taken, 1)
                dve.wait_ge(k_taken, c + 1)
                k.then(nc.vector.tensor_reduce(amax[:, :], heads(kf[:, :, :]), AX.X, ALU.max,
                                               apply_absolute_value=True))
                k.then(nc.vector.tensor_scalar(kscale[:, :], amax[:, :], 1.0 / 127.0, QMIN, ALU.mult, ALU.max))
                k.then(nc.vector.reciprocal(kinv[:, :], kscale[:, :]))
                k.then(nc.vector.tensor_tensor(heads(kr[:, :, :]), heads(kf[:, :, :]), last_axis(kinv[:, :], HD),
                                               ALU.mult))
                k.then(nc.vector.tensor_scalar(kr[:, :, :], kr[:, :, :], ROUND, ROUND, ALU.add, ALU.subtract))
                if not (isinstance(c, int) and c < 2):
                    dve.wait_ge(res_done, c - 1)
                nc.vector.tensor_tensor(heads(kq[:, par]), heads(kr[:, :, :]), last_axis(kscale[:, :], HD),
                                        ALU.mult).then_inc(kq_ready, 1)
                dve.wait_ge(v_ready, c + 1)
                nc.vector.tensor_tensor(vf[0:rows, bass.ds(4 * c, 4), :], pv[0:rows, :, :],
                                        middle_axis(bkv[0:rows, D:2 * D], 4), ALU.add).then_inc(v_taken, 1)

            quantise(0, 0, P)
            quantise(1, 1, P)
            with dve.Fori(1, NKC // 2) as i:
                for par in range(2):
                    quantise(2 * i + par, par, P)
            quantise(NKC, 0, TAILW)

            v = Steps(dve, vsteps)
            dve.wait_ge(v_taken, NKC + 1)
            v.then(nc.vector.tensor_reduce(vmax[:, :], vf[:, :, :].rearrange("p t d -> p d t"), AX.X, ALU.max,
                                           apply_absolute_value=True))
            dve.wait_ge(v_turned, 1)
            v.then(nc.vector.tensor_reduce(vcol[:, :], pk[:, 0, :].rearrange("p (k n) -> p k n", k=KD), AX.X, ALU.max))
            for k in range(KD):
                done = nc.vector.tensor_scalar(vdiag[:, k, :], ident[:, :], vcol[:, k:k + 1], None, ALU.mult)
            done.then_inc(v_diag, 1)
            dve.wait_ge(v_bcast, 1)
            v.then(nc.vector.tensor_scalar(sv[:, :], pk[:, 2, :], 1.0 / 127.0, QMIN, ALU.mult, ALU.max))
            v.then(nc.vector.reciprocal(vinv[:, :], sv[:, :]))
            for n in range(4):
                cols = slice(4 * n * HD, 4 * (n + 1) * HD)
                v.then(nc.vector.tensor_tensor(vr[:, :, :], vf[:, :, cols], middle_axis(vinv[:, cols], VT), ALU.mult))
                if n >= 2:
                    dve.wait_ge(v_stored[n % 2], 16)
                for hh in range(4):
                    done = nc.vector.tensor_scalar(vint[:, n % 2, hh], vr[:, :, hh * HD:(hh + 1) * HD],
                                                   ROUND, ROUND, ALU.add, ALU.subtract)
                done.then_inc(vint_ready, 1)
                dve.wait_ge(vint_ready, n + 1)


def attention(nc, keep, scratch):
    ident, sq, o, sums = keep["ident"], keep["sq"], keep["o"], keep["sums"]
    kT_d, qT_d, v_d = scratch
    LOOP = 8
    LAG_T, LAG_PV = 2, 3
    with ExitStack() as ctx:
        def sb(name, shape, dt=F32):
            return ctx.enter_context(nc.sbuf_tensor(name, shape, dt))

        def psum(name, shape, dt=F32):
            return ctx.enter_context(nc.psum_tensor(name, shape, dt))

        def sem(name):
            return ctx.enter_context(nc.semaphore(name))

        kT = sb("kT", [P, 2, NK], BF16)
        qT = sb("qT", [P, 2, 2 * P], BF16)
        v = sb("v_head", [P, 2, VT, HD], BF16)
        s = sb("s", [P, 2, NK])
        e8 = sb("e8", [P, 2, NK], U8)
        words = sb("words", [P, 2, NKC + 1, P], U32)
        pT = sb("pT", [P, 2, VT, P], BF16)
        smax = sb("smax", [P, 2, NSC])
        nmax = sb("nmax", [P, 2])
        bias = sb("bias", [P, 2])

        ps = psum("ps", [P, 2, SC])
        pw = psum("pw", [P, 3, KC])
        po = psum("po", [P, KC])

        heads_in = [sem("heads_in0"), sem("heads_in1")]
        v_in = [sem("v_in0"), sem("v_in1")]
        const = sem("const")
        scored = sem("scored")
        copied = sem("copied")
        max_ready = sem("max_ready")
        bias_ready = sem("bias_ready")
        exped = sem("exped")
        turned = sem("turned")
        wordsd = sem("wordsd")
        unpacked = sem("unpacked")
        weighed = sem("weighed")
        o_taken = sem("o_taken")
        pool_passed = sem("pool_passed")

        sqf = sq[:, :, :].rearrange("p s j -> p (s j)")

        block = ctx.enter_context(nc.Block())

        def first(n):
            return isinstance(n, int) and n < 2

        @block.sync
        def _(sp):
            def load_heads(st, par, head, group):
                if not first(st):
                    sp.wait_ge(scored, 2 * NSC * (st - 1))
                sp.dma_start(kT[0:QR, par, :],
                             kT_d[bass.ds(head, 1)].rearrange("o r n -> (o r) n")).then_inc(heads_in[par], 16)
                sp.dma_start(qT[0:QR, par, :],
                             qT_d[bass.ds(head, 1), :, bass.ds(group * 2 * P, 2 * P)]
                             .rearrange("o r n -> (o r) n")).then_inc(heads_in[par], 16)

            def load_v(st, par, head):
                if not first(st):
                    sp.wait_ge(weighed, 2 * (st - 1))
                sp.dma_start(v[:, par].rearrange("p t d -> p (t d)"),
                             v_d[bass.ds(head, 1)].rearrange("o p n -> (o p) n")).then_inc(v_in[par], 16)

            sp.wait_ge(const, 2)
            load_heads(0, 0, 0, 0)
            load_heads(1, 1, 1, 0)
            load_v(0, 0, 0)
            load_heads(2, 0, 2, 0)
            load_v(1, 1, 1)
            load_heads(3, 1, 3, 0)
            load_v(2, 0, 2)
            with sp.Fori(2, STEPS // 2) as i:
                group, hp = i // (H // 2), i % (H // 2)
                load_heads(2 * i, 0, 2 * hp, group)
                load_v(2 * i - 1, 1, (2 * hp + H - 1) % H)
                load_heads(2 * i + 1, 1, 2 * hp + 1, group)
                load_v(2 * i, 0, 2 * hp)
            load_v(STEPS - 1, 1, H - 1)
            for par in range(2):
                sp.wait_ge(heads_in[par], 32 * (STEPS // 2))
                sp.wait_ge(v_in[par], 16 * (STEPS // 2))

        @block.tensor
        def _(pe):
            def scores(u, par, j, early, c):
                a, w = SCS[c]
                n = NSC * u + c
                if not (early and u == 0 and c < 2):
                    pe.wait_ge(copied, n - 1)
                if c == 1 and not (early and u < LAG_T + 1):
                    pe.wait_ge(wordsd, WG * (u - LAG_T))
                for b in range(a, a + w, KC):
                    m = min(KC, a + w - b)
                    mm = nc.tensor.matmul(ps[:, buffer(j, c), b - a:b - a + m], qT[:, par, j * P:(j + 1) * P],
                                          kT[:, par, b:b + m], start=True, stop=True)
                mm.then_inc(scored, 1)

            def buffer(j, c):
                return (NSC * j + c) % 2

            def turn(w_, j, g, early):
                if g == 0:
                    pe.wait_ge(exped, w_ + 1)
                if g < WG - 1:
                    if not early:
                        pe.wait_ge(wordsd, WG * (w_ - 1) + g + 1)
                    out = pw[:, g, :]
                else:
                    out = ps[:, buffer(j, NSC - 1), KC:2 * KC]
                ew = e8[:, j, :].bitcast(F32)
                for t in range(4 * g, min(4 * g + 4, NKC + 1)):
                    m = min(P, NK // 4 - t * P)
                    mm = nc.tensor.transpose(out[0:m, (t % 4) * P:(t % 4 + 1) * P], ew[:, t * P:t * P + m],
                                             ident[:, :])
                mm.then_inc(turned, 1)

            def weigh(w_, k, steps, g, early):
                par, j = k // 2, k % 2
                if g == 0:
                    pe.wait_ge(v_in[par], 16 * steps)
                    if not (early and w_ == 0):
                        pe.wait_ge(o_taken, w_)
                pe.wait_ge(unpacked, WG * w_ + g + 1)
                for t in range(16 * g, min(16 * g + 16, VT)):
                    m = min(P, NK // 4 - (t // 4) * P)
                    mm = nc.tensor.matmul(po[:, 0:HD], pT[0:m, j, t, :], v[0:m, par, t, :],
                                          start=(t == 0), stop=(t == VT - 1))
                if g == WG - 1:
                    mm.then_inc(weighed, 1)

            def unit(i, k, early=False):
                u, par, j = 4 * i + k, k // 2, k % 2
                turns = not early or u >= LAG_T
                weighs = not early or u >= LAG_PV
                kv = (k - LAG_PV) % 4
                steps = i + 1 if k >= LAG_PV else i
                if j == 0:
                    pe.wait_ge(heads_in[par], 32 * (i + 1))
                for c in range(NSC):
                    scores(u, par, j, early, c)
                    if turns and c < WG - 1:
                        turn(u - LAG_T, j, c, early and u == LAG_T)
                    if turns and c == NSC - 1:
                        turn(u - LAG_T, j, WG - 1, early)
                    if weighs and 3 <= c <= 5:
                        weigh(u - LAG_PV, kv, steps, c - 3, early)
                    if weighs and c == 5:
                        weigh(u - LAG_PV, kv, steps, WG - 1, early)

            for k in range(4):
                unit(0, k, True)
            with pe.Fori(1, UNITS // 4) as i:
                for k in range(4):
                    unit(i, k)
            pe.wait_ge(copied, NSC * UNITS)
            for u in range(UNITS, UNITS + LAG_PV):
                if u < UNITS + LAG_T:
                    for g in range(WG):
                        if g == WG - 1 and u > UNITS:
                            pe.wait_ge(wordsd, WG * (u - LAG_T))
                        turn(u - LAG_T, u % 2, g, False)
                w_ = u - LAG_PV
                for g in range(WG):
                    weigh(w_, w_ % 4, w_ // 4 + 1, g, False)

        @block.scalar
        def _(act):
            def exp(u, j, early):
                act.wait_ge(bias_ready, u + 1)
                if not early:
                    act.wait_ge(turned, WG * (u - 1))
                nc.scalar.activation(e8[:, j, :], s[:, j, :], ACT.Exp, bias=bias[:, j:j + 1],
                                     scale=sqf[:, bass.ds(u, 1)], accum_out=sums[:, bass.ds(u, 1)]).then_inc(exped, 1)

            def take_words(w_, j, early):
                if not early:
                    act.wait_ge(unpacked, WG * (w_ - 1))
                for g in range(WG):
                    act.wait_ge(turned, WG * w_ + g + 1)
                    if g < WG - 1:
                        nc.scalar.copy(words[:, j, 4 * g:4 * g + 4, :].rearrange("p t q -> p (t q)"),
                                       pw[:, g, :].bitcast(U32)).then_inc(wordsd, 1)
                    else:
                        nc.scalar.copy(words[0:TAILW, j, NKC, :],
                                       ps[0:TAILW, (NSC * j + NSC - 1) % 2, KC:KC + P].bitcast(U32)).then_inc(wordsd, 1)

            exp(0, 0, True)
            exp(1, 1, True)
            take_words(0, 0, True)
            exp(2, 0, False)
            take_words(1, 1, True)
            exp(3, 1, False)
            for u in range(4, LOOP):
                take_words(u - 2, u % 2, False)
                exp(u, u % 2, False)
            with act.Fori(1, UNITS // LOOP) as i:
                for k in range(LOOP):
                    take_words(LOOP * i + k - 2, k % 2, False)
                    exp(LOOP * i + k, k % 2, False)
            for j in range(2):
                take_words(UNITS - 2 + j, j, False)

        @block.gpsimd
        def _(pool):
            def unpack(w_, j, early):
                if not early:
                    pool.wait_ge(weighed, w_ - 1)
                for g in range(WG):
                    pool.wait_ge(wordsd, WG * w_ + g + 1)
                    pool.sem_inc(pool_passed, 1)
                    m, a, b = (P, 4 * g, 4 * g + 4) if g < WG - 1 else (TAILW, NKC, NKC + 1)
                    nc.gpsimd.tensor_scalar(
                        pT[0:m, j, 4 * a:4 * b, :].rearrange("p (t b) q -> p t b q", b=4),
                        words[0:m, j, a:b, :].bitcast(U8).rearrange("p t (q b) -> p t b q", b=4),
                        1.0, 0.0, ALU.mult, ALU.add).then_inc(unpacked, 1)

            for w_ in range(LOOP):
                unpack(w_, w_ % 2, w_ < 2)
            with pool.Fori(1, UNITS // LOOP) as i:
                for k in range(LOOP):
                    unpack(LOOP * i + k, k % 2, False)

        @block.vector
        def _(dve):
            nc.vector.memset(kT[:, :, :].rearrange("p a n -> p (a n)").bitcast(U32), 0).then_inc(const, 1)
            nc.vector.memset(qT[:, :, :].rearrange("p a n -> p (a n)").bitcast(U32), 0).then_inc(const, 1)

            def take_o(w_):
                dve.wait_ge(weighed, w_ + 1)
                nc.vector.tensor_copy(o[:, bass.ds(w_ * HD, HD)], po[:, 0:HD]).then_inc(o_taken, 1)

            def unit(u, j, early):
                if not (early and u < 2):
                    dve.wait_ge(exped, u - 1)
                for c, (a, w) in enumerate(SCS):
                    dve.wait_ge(scored, NSC * u + c + 1)
                    nc.vector.tensor_scalar(s[:, j, a:a + w], ps[:, (NSC * j + c) % 2, 0:w], 1.0, None,
                                            ALU.mult, ALU.max, accum_out=smax[:, j, c:c + 1]).then_inc(copied, 1)
                dve.wait_ge(copied, NSC * (u + 1))
                nc.vector.tensor_reduce(nmax[:, j:j + 1], smax[:, j, :], AX.X, ALU.max, negate=True).then_inc(max_ready, 1)
                if not (early and u < LAG_PV):
                    take_o(u - LAG_PV)
                dve.wait_ge(max_ready, u + 1)
                nc.vector.tensor_scalar(bias[:, j:j + 1], nmax[:, j:j + 1], sqf[:, bass.ds(u, 1)], LN255,
                                        ALU.mult, ALU.add).then_inc(bias_ready, 1)

            for u in range(LOOP):
                unit(u, u % 2, True)
            with dve.Fori(1, UNITS // LOOP) as i:
                for k in range(LOOP):
                    unit(LOOP * i + k, k % 2, False)
            for w_ in range(UNITS - LAG_PV, UNITS):
                take_o(w_)


def ffn(nc, io, keep):
    x, ident, sv, o, sums = keep["x"], keep["ident"], keep["sv"], keep["o"], keep["sums"]
    with ExitStack() as ctx:
        def sb(name, shape, dt=F32):
            return ctx.enter_context(nc.sbuf_tensor(name, shape, dt))

        def psum(name, shape, dt=F32):
            return ctx.enter_context(nc.psum_tensor(name, shape, dt))

        def sem(name):
            return ctx.enter_context(nc.semaphore(name))

        wp = sb("wp", [P, KD, D])
        bp = sb("bp", [P, D])
        gates = sb("gates", [P, 2])
        tgates = sb("tgates", [P, 2])
        rsum = sb("rsum", [P, UNITS])
        on = sb("on", [P, QT, D])
        xT = sb("xT", [P, KD, NQ])
        hT_hi = sb("hT_hi", [P, KD, NQ], F32R)
        hT_lo = sb("hT_lo", [P, KD, NQ], F32R)
        y = sb("y", [P, QT, D])
        stats = sb("stats2", [P, QT, 6])
        mv = sb("mv2", [P, QT, 2])
        ln = sb("ln2", [P, 4, QT])
        router = sb("router", [P, KD, RW])
        router_hi = sb("router_hi", [P, KD, RW], F32R)
        router_lo = sb("router_lo", [P, KD, RW], F32R)
        lmax = sb("lmax", [P, QT])
        probs = sb("probs", [P, QT, E])
        psums = sb("psums", [P, QT])
        top = sb("top", [P, QT, TOPK])
        rest = sb("rest", [P, QT, E])
        sig = sb("sig", [P, QT])
        share = sb("share", [P, QT, E + 1])
        PIECE, WP = 2 * EG * I, KD + 1
        weights = sb("weights", [P, 2, WP, PIECE])
        weights_hi = sb("weights_hi", [P, 2, WP, PIECE], F32R)
        weights_lo = sb("weights_lo", [P, 2, WP, PIECE], F32R)
        th = sb("th", [P, 2, EG * I])
        gl = sb("gl", [P, 2, EG * I])
        gu = sb("gu", [P, 2, EG * I])
        act_in = sb("act_in", [P, 2, EG * I])
        aT_hi = sb("aT_hi", [P, 2, 2 * P], F32R)
        aT_lo = sb("aT_lo", [P, 2, 2 * P], F32R)

        pacc = psum("pacc", [P, QT, D])
        pgu = psum("pgu", [P, 2, 2 * EG * I])
        pat = psum("pat", [P, 2, KC])
        wide = pacc[:, :, :].rearrange("p t d -> p (t d)")

        loaded = sem("loaded3")
        tanhs = sem("tanhs")
        steps = sem("steps3")
        o_ready = sem("o_ready")
        turned = sem("turned3")
        xT_ready = sem("xT_ready")
        hT_high = sem("hT_high")
        hT_ready = sem("hT_ready3")
        root = sem("root3")
        proj = sem("proj")
        h_ready = sem("h_ready3")
        routed = sem("routed")
        shifted = sem("shifted")
        exped = sem("exped3")
        share_ready = sem("share_ready")
        w_in = [sem("w_in0"), sem("w_in1")]
        w_hi = sem("w_hi")
        w_split = sem("w_split")
        router_split = sem("router_split")
        gu_ready = sem("gu_ready")
        th_ready = sem("th_ready")
        gl_ready = sem("gl_ready")
        gu_done = sem("gu_done")
        a_ready = sem("a_ready")
        a_turned = sem("a_turned")
        aT_high = sem("aT_high")
        aT_ready = sem("aT_ready")
        added = sem("added")
        y_ready = sem("y_ready")
        out_done = sem("out_done")

        block = ctx.enter_context(nc.Block())
        NU = (NEG + 1) * QT
        LAG_T, LAG_D = 2, 3
        SPLIT_AT = (3, 4, 5)

        @block.sync
        def _(sp):
            for dst, src in ((wp[:, :, :], io["Wp"].rearrange("(k p) n -> p k n", p=P)),
                             (bp[:, :], io["bp"].broadcast_to([P, D])),
                             (gates[:, 0:1], io["g_xattn"].broadcast_to([P, 1])),
                             (gates[:, 1:2], io["g_ffn"].broadcast_to([P, 1])),
                             (router[:, :, :], io["router"].rearrange("(k p) n -> p k n", p=P))):
                sp.dma_start(dst, src).then_inc(loaded, 16)

            def load(g, par):
                sp.dma_start(weights[:, par, 0:KD, :], io["gate_up"][bass.ds(g, 1)].rearrange("o (k p) n -> p (o k) n", p=P))\
                  .then_inc(w_in[par], 16)
                sp.dma_start(weights[:, par, KD, :].rearrange("p (k n) -> p k n", k=2),
                             io["down"][bass.ds(g, 1)].rearrange("o (k p) n -> p (o k) n", p=P)).then_inc(w_in[par], 16)

            load(0, 0)
            load(1, 1)
            with sp.Fori(1, NEG // 2) as i:
                for par in range(2):
                    g = 2 * i + par
                    sp.wait_ge(w_split, WP * (g - 1))
                    load(g, par)
            sp.wait_ge(w_split, WP * (NEG - 1))
            sp.dma_start(weights[:, 0, 0:KD, 0:2 * I],
                         io["shared_gate_up"].rearrange("(k p) n -> p k n", p=P)).then_inc(w_in[0], 16)
            sp.dma_start(weights[0:I, 0, KD, 0:D], io["shared_down"]).then_inc(w_in[0], 16)
            out = io["out"].rearrange("(t p) d -> p t d", p=P)
            for half in range(2):
                sp.wait_ge(y_ready, half + 1)
                sp.dma_start(out[:, 4 * half:4 * half + 4, :], y[:, 4 * half:4 * half + 4, :]).then_inc(out_done, 16)
            sp.wait_ge(out_done, 32)

        @block.tensor
        def _(pe):
            def turn_rows(src):
                for k in range(KD):
                    for t in range(QT):
                        mm = nc.tensor.transpose(wide[:, k * NQ + t * P:k * NQ + (t + 1) * P],
                                                 src[:, t, k * P:(k + 1) * P], ident[:, :])
                    mm.then_inc(turned, 1)

            pe.wait_ge(loaded, 16 * 5)
            pe.wait_ge(o_ready, 1)
            turn_rows(on)
            pe.wait_ge(xT_ready, 2)
            for t in range(QT):
                for k in range(KD):
                    mm = nc.tensor.matmul(pacc[:, t, :], xT[:, k, t * P:(t + 1) * P], wp[:, k, :],
                                          start=(k == 0), stop=(k == KD - 1))
            mm.then_inc(proj, 1)
            pe.wait_ge(h_ready, 1)
            turn_rows(on)
            pe.wait_ge(hT_ready, KD)
            pe.wait_ge(router_split, 2)
            for t in range(QT):
                for k in range(KD):
                    mm = product(nc, pat[:, t // 4, (t % 4) * P:(t % 4) * P + RW],
                                 [h[:, k, t * P:(t + 1) * P] for h in (hT_hi, hT_lo)],
                                 [r[:, k, :] for r in (router_hi, router_lo)], start=(k == 0), stop=(k == KD - 1))
            mm.then_inc(routed, 1)

            def gate_up(n, g, g_par, t, early, width=2 * EG * I):
                if t == 0:
                    pe.wait_ge(w_split, WP * g + KD)
                if not (early and n < 2):
                    pe.wait_ge(gu_done, n - 1)
                for k in range(KD):
                    mm = product(nc, pgu[:, t % 2, 0:width], [h[:, k, t * P:(t + 1) * P] for h in (hT_hi, hT_lo)],
                                 [w[:, g_par, k, 0:width] for w in (weights_hi, weights_lo)],
                                 start=(k == 0), stop=(k == KD - 1))
                mm.then_inc(gu_ready, 1)

            def turn(n, b, early, width=EG * I):
                pe.wait_ge(a_ready, n + 1)
                if not (early and n < 2):
                    pe.wait_ge(aT_ready, n - 1)
                for k in range(-(-width // P)):
                    m = min(P, width - k * P)
                    mm = nc.tensor.transpose(pat[0:m, b, k * P:(k + 1) * P], act_in[:, b, k * P:k * P + m], ident[:, :])
                mm.then_inc(a_turned, 1)

            def add(n, b, g, t, g_par, width=EG * I):
                if t == 0:
                    pe.wait_ge(w_split, WP * (g + 1))
                pe.wait_ge(aT_ready, n + 1)
                for k in range(-(-width // P)):
                    m = min(P, width - k * P)
                    mm = product(nc, pacc[:, t, :], [a[0:m, b, k * P:(k + 1) * P] for a in (aT_hi, aT_lo)],
                                 [w[0:m, g_par, KD, k * D:(k + 1) * D] for w in (weights_hi, weights_lo)],
                                 start=False, stop=False, skip_group_check=True)
                mm.then_inc(added, 1)

            def group(base, g, g_par, early, last=False):
                for t in range(QT):
                    n = base + t
                    gate_up(n, g, g_par, t, early, 2 * I if last else 2 * EG * I)
                    if not (early and n < LAG_T):
                        turn(n - LAG_T, t % 2, early, I if last and t >= LAG_T else EG * I)
                    if not (early and n < LAG_D):
                        same = t >= LAG_D
                        add(n - LAG_D, (t - LAG_D) % 2, g if same else g - 1, (t - LAG_D) % QT,
                            g_par if same else 1 - g_par, I if last and same else EG * I)

            pe.wait_ge(share_ready, 1)
            group(0, 0, 0, True)
            group(QT, 1, 1, False)
            with pe.Fori(1, NEG // 2) as i:
                for par in range(2):
                    group(2 * QT * i + QT * par, 2 * i + par, par, False)
            group(NEG * QT, NEG, 0, False, last=True)
            for t in range(LAG_D):
                n = NU + t
                if t < LAG_T:
                    turn(n - LAG_T, t % 2, False, I)
                add(n - LAG_D, (n - LAG_D) % 2, NEG, QT - LAG_D + t, 0, I)

        @block.scalar
        def _(act):
            act.wait_ge(loaded, 16 * 5)
            nc.scalar.activation(tgates[:, :], gates[:, :], ACT.Tanh).then_inc(tanhs, 1)

            def split_weights(g, par, piece):
                if piece == 0:
                    act.wait_ge(w_in[par], 32 * (g // 2 + 1))
                    if not (isinstance(g, int) and g < 2):
                        act.wait_ge(gu_ready, QT * (g - 1))
                if piece == KD and not (isinstance(g, int) and g < 2):
                    act.wait_ge(added, QT * (g - 1))
                nc.scalar.copy(weights_hi[:, par, piece, :], weights[:, par, piece, :]).then_inc(w_hi, 1)

            for k in range(KD):
                act.wait_ge(turned, k + 1)
                nc.scalar.copy(xT[:, k, :], wide[:, k * NQ:(k + 1) * NQ]).then_inc(xT_ready, 1)
            nc.scalar.copy(router_hi[:, :, :], router[:, :, :]).then_inc(router_split, 1)
            for g in range(2):
                for piece in range(WP):
                    split_weights(g, g, piece)
            act.wait_ge(steps, BEFORE_LN + VAR_STEP)
            nc.scalar.activation(ln[:, 1, :], ln[:, 0, :], ACT.Sqrt).then_inc(root, 1)
            for k in range(KD):
                act.wait_ge(turned, KD + k + 1)
                nc.scalar.copy(hT_hi[:, k, :], wide[:, k * NQ:(k + 1) * NQ]).then_inc(hT_high, 1)
            act.wait_ge(shifted, 1)
            nc.scalar.activation(probs[:, :, :], probs[:, :, :], ACT.Exp).then_inc(exped, 1)
            nc.scalar.activation(sig[:, :], sig[:, :], ACT.Tanh, scale=0.5).then_inc(exped, 1)

            def tanh(n, b, early, width=EG * I):
                act.wait_ge(gu_ready, n + 1)
                if not (early and n < 2):
                    act.wait_ge(gl_ready, n - 1)
                nc.scalar.activation(th[:, b, 0:width], pgu[:, b, 0:width], ACT.Tanh, scale=0.5).then_inc(th_ready, 1)

            def take(n, b, early, width=EG * I):
                act.wait_ge(a_turned, n + 1)
                if not (early and n < 2):
                    act.wait_ge(added, n - 1)
                m, w = (P, width) if width > P else (width, P)
                nc.scalar.copy(aT_hi[0:m, b, 0:w], pat[0:m, b, 0:w]).then_inc(aT_high, 1)

            def unit(n, g, par, t):
                tanh(n, t % 2, False)
                take(n - 2, t % 2, False)
                if t in SPLIT_AT:
                    split_weights(g + 1, 1 - par, SPLIT_AT.index(t))

            tanh(0, 0, True)
            tanh(1, 1, True)
            for n in range(2, 4):
                tanh(n, n % 2, False)
                take(n - 2, n % 2, True)
            for n in range(4, QT):
                tanh(n, n % 2, False)
                take(n - 2, n % 2, False)
            for t in range(QT):
                unit(QT + t, 1, 1, t)
            with act.Fori(1, NEG // 2) as i:
                for par in range(2):
                    for t in range(QT):
                        unit(2 * QT * i + QT * par + t, 2 * i + par, par, t)
            for n in range(NEG * QT, NU + 2):
                if n < NU:
                    tanh(n, n % 2, False, I)
                take(n - 2, n % 2, False, I if n - 2 >= NEG * QT else EG * I)

        @block.gpsimd
        def _(pool):
            def weigh(n, b, t, col, early, experts=EG):
                pool.wait_ge(gu_done, n + 1)
                if not (early and n < 2):
                    pool.wait_ge(a_turned, n - 1)
                w = experts * I
                nc.gpsimd.tensor_tensor(act_in[:, b, 0:w].rearrange("p (e i) -> p e i", e=experts),
                                        gu[:, b, 0:w].rearrange("p (e i) -> p e i", e=experts),
                                        last_axis(share[:, t, bass.ds(col, experts)], I), ALU.mult).then_inc(a_ready, 1)

            def rest_of(par, piece, g):
                pool.wait_ge(w_hi, WP * g + piece + 1)
                nc.gpsimd.tensor_tensor(weights_lo[:, par, piece, :], weights[:, par, piece, :],
                                        weights_hi[:, par, piece, :].bitcast(F32), ALU.subtract).then_inc(w_split, 1)

            def group(g, par, early=False):
                for t in range(QT):
                    weigh(QT * g + t, t % 2, t, EG * g, early)
                    if t in SPLIT_AT and not early:
                        rest_of(1 - par, SPLIT_AT.index(t), g + 1)

            for g in range(2):
                for piece in range(WP):
                    rest_of(g, piece, g)
            pool.wait_ge(share_ready, 1)
            group(0, 0, True)
            group(1, 1)
            with pool.Fori(1, NEG // 2) as i:
                for par in range(2):
                    group(2 * i + par, par)
            for t in range(QT):
                weigh(NEG * QT + t, t % 2, t, E, False, 1)

        @block.vector
        def _(dve):
            c = Steps(dve, steps)
            dve.wait_ge(loaded, 16 * 5)
            c.then(nc.vector.reciprocal(rsum[:, :], sums[:, :]))
            c.then(nc.vector.tensor_tensor(o[:, :].rearrange("p (u d) -> p u d", d=HD),
                                           o[:, :].rearrange("p (u d) -> p u d", d=HD),
                                           last_axis(rsum[:, :], HD), ALU.mult))
            ov = o[:, :].rearrange("p (g h j d) -> p g j h d", h=H, j=2, d=HD)
            for t in range(QT):
                done = nc.vector.tensor_tensor(on[:, t, :].rearrange("p (h d) -> p h d", h=H), ov[:, t // 2, t % 2],
                                               sv[:, :].rearrange("p (h d) -> p h d", h=H), ALU.mult)
            done.then_inc(o_ready, 1)
            dve.wait_ge(proj, 1)
            dve.wait_ge(tanhs, 1)
            c.then(nc.vector.tensor_tensor(y[:, :, :], pacc[:, :, :], middle_axis(bp[:, :], QT), ALU.add))
            c.then(nc.vector.scalar_tensor_tensor(x[:, :, :], y[:, :, :], tgates[:, 0:1], x[:, :, :], ALU.mult, ALU.add))
            assert c.n == BEFORE_LN
            layernorm(nc, dve, Steps(dve, steps, BEFORE_LN), x, stats, mv, ln, on, root, h_ready)
            c.n += LN_STEPS

            dve.wait_ge(router_split, 1)
            nc.vector.tensor_tensor(router_lo[:, :, :], router[:, :, :], router_hi[:, :, :].bitcast(F32),
                                    ALU.subtract).then_inc(router_split, 1)
            for k in range(KD):
                dve.wait_ge(hT_high, k + 1)
                nc.vector.tensor_tensor(hT_lo[:, k, :], wide[:, k * NQ:(k + 1) * NQ], hT_hi[:, k, :].bitcast(F32),
                                        ALU.subtract).then_inc(hT_ready, 1)

            dve.wait_ge(routed, 1)
            logits = pat[:, :, :].rearrange("p b (t n) -> p (b t) n", n=P)
            c.then(nc.vector.tensor_reduce(lmax[:, :], logits[:, :, 0:E], AX.X, ALU.max))
            nc.vector.tensor_copy(sig[:, :], logits[:, :, E])
            nc.vector.tensor_tensor(probs[:, :, :], logits[:, :, 0:E], last_axis(lmax[:, :], E),
                                    ALU.subtract).then_inc(shifted, 1)
            nc.vector.memset(pacc[:, :, :], 0.0)
            dve.wait_ge(exped, 2)
            c.then(nc.vector.tensor_reduce(psums[:, :], probs[:, :, :], AX.X, ALU.add))
            c.then(nc.vector.reciprocal(psums[:, :], psums[:, :]))
            c.then(nc.vector.tensor_tensor(probs[:, :, :], probs[:, :, :], last_axis(psums[:, :], E), ALU.mult))
            for t in range(QT):
                done = nc.vector.max(top[:, t, :], probs[:, t, :])
            c.then(done)
            for t in range(QT):
                done = nc.vector.match_replace(rest[:, t, :], top[:, t, :], probs[:, t, :], -1.0)
            c.then(done)
            c.then(nc.vector.tensor_reduce(lmax[:, :], top[:, :, :], AX.X, ALU.add))
            c.then(nc.vector.reciprocal(lmax[:, :], lmax[:, :]))
            c.then(nc.vector.tensor_scalar(lmax[:, :], lmax[:, :], 0.5, None, ALU.mult))
            c.then(nc.vector.scalar_tensor_tensor(probs[:, :, :], rest[:, :, :], 0.0, probs[:, :, :], ALU.is_lt, ALU.mult))
            nc.vector.tensor_tensor(share[:, :, 0:E], probs[:, :, :], last_axis(lmax[:, :], E), ALU.mult)
            nc.vector.tensor_scalar(share[:, :, E], sig[:, :], 1.0, 0.25, ALU.add, ALU.mult).then_inc(share_ready, 1)

            def times(n, b, early, width=EG * I):
                dve.wait_ge(th_ready, n + 1)
                if not (early and n < 1):
                    dve.wait_ge(gu_done, n)
                nc.vector.scalar_tensor_tensor(gl[:, b, 0:width], th[:, b, 0:width], 1.0, pgu[:, b, 0:width],
                                               ALU.add, ALU.mult).then_inc(gl_ready, 1)
                dve.wait_ge(gl_ready, n + 1)
                if not (early and n < 2):
                    dve.wait_ge(a_ready, n - 1)
                nc.vector.tensor_tensor(gu[:, b, 0:width], gl[:, b, 0:width], pgu[:, b, width:2 * width],
                                        ALU.mult).then_inc(gu_done, 1)

            def rest_of(n, b, early, width=EG * I):
                dve.wait_ge(aT_high, n + 1)
                if not (early and n < 2):
                    dve.wait_ge(added, n - 1)
                m, w = (P, width) if width > P else (width, P)
                nc.vector.tensor_tensor(aT_lo[0:m, b, 0:w], pat[0:m, b, 0:w], aT_hi[0:m, b, 0:w].bitcast(F32),
                                        ALU.subtract).then_inc(aT_ready, 1)

            for n in range(4):
                times(n, n % 2, n < 2)
                if n >= 2:
                    rest_of(n - 2, n % 2, True)
            with dve.Fori(2, NEG * QT // 2) as i:
                for b in range(2):
                    times(2 * i + b, b, False)
                    rest_of(2 * i + b - 2, b, False)
            for n in range(NEG * QT, NU + 2):
                if n < NU:
                    times(n, n % 2, False, I)
                rest_of(n - 2, n % 2, False, I if n - 2 >= NEG * QT else EG * I)
            dve.wait_ge(added, NU)
            for half in range(2):
                ts = slice(4 * half, 4 * half + 4)
                nc.vector.scalar_tensor_tensor(y[:, ts, :], pacc[:, ts, :], tgates[:, 1:2], x[:, ts, :],
                                               ALU.mult, ALU.add).then_inc(y_ready, 1)


def program(nc, io):
    with ExitStack() as ctx:
        def sb(name, shape, dt=F32):
            return ctx.enter_context(nc.sbuf_tensor(name, shape, dt))

        keep = {
            "x": sb("x", [P, QT, D]),
            "ident": sb("ident", [P, P]),
            "sq": sb("sq", [P, STEPS, 2]),
            "sv": sb("sv", [P, D]),
            "o": sb("o", [P, UNITS * HD]),
            "sums": sb("sums", [P, UNITS]),
        }
        scratch = (nc.dram_tensor("kT_parts", (H, QR, NK), BF16, kind="Internal").ap(),
                   nc.dram_tensor("qT_parts", (H, QR, NQ), BF16, kind="Internal").ap(),
                   nc.dram_tensor("v_ints", (H, P, VT * HD), BF16, kind="Internal").ap())
        projections(nc, io, keep, scratch)
        attention(nc, keep, scratch)
        ffn(nc, io, keep)


def kernel(**inputs):
    import numpy as np
    import concourse.bacc as bacc
    from concourse.bass_utils import run_bass_kernel_spmd

    g = {k: np.asarray(a) for k, a in inputs.items()}
    gu = g["L0_ffn_gate_up_proj"].reshape(NEG, EG, 2, I, D)
    arrays = {
        "x": g["x"].reshape(NQ, D),
        "ctxT": g["ctx_2048"].reshape(NK, D).T,
        "eye": np.eye(P, dtype=np.float32),
        "Wq": g["L0_xattn_Wq"], "bq": g["L0_xattn_bq"].reshape(1, D),
        "Wkv": g["L0_xattn_Wkv"], "bkv": g["L0_xattn_bkv"].reshape(1, 2 * D),
        "Wp": g["L0_xattn_Wp"], "bp": g["L0_xattn_bp"].reshape(1, D),
        "g_xattn": g["g_xattn"].reshape(1, 1), "g_ffn": g["g_ffn"].reshape(1, 1),
        "router": np.concatenate([g["L0_ffn_router_w"], g["L0_ffn_shared_expert_gate_w"],
                                  g["L0_ffn_shared_expert_gate_w"]], 0).T,
        "gate_up": gu.transpose(0, 4, 2, 1, 3).reshape(NEG, D, 2 * EG * I),
        "down": g["L0_ffn_down_proj"].transpose(0, 2, 1).reshape(NEG, EG * I, D),
        "shared_gate_up": np.concatenate([g["L0_ffn_shared_gate_w"], g["L0_ffn_shared_up_w"]], 0).T,
        "shared_down": g["L0_ffn_shared_down_w"].T,
    }
    nc = bacc.Bacc("TRN2", target_bir_lowering=False, num_devices=1)
    io, feed = {}, {}
    for name, a in arrays.items():
        feed[f"in_{name}"] = np.ascontiguousarray(a)
        io[name] = nc.dram_tensor(f"in_{name}", a.shape, mybir.dt.from_np(a.dtype), kind="ExternalInput").ap()
    io["out"] = nc.dram_tensor("out_x", (NQ, D), F32, kind="ExternalOutput").ap()
    program(nc, io)
    r = run_bass_kernel_spmd(nc, [feed], core_ids=[0])
    return r.results[0]["out_x"].reshape(4, NQ // 4, D)
```

```python
from contextlib import ExitStack

import concourse.bass as bass
from concourse import mybir

F32 = mybir.dt.float32
F32R = mybir.dt.float32r
BF16 = mybir.dt.bfloat16
U8 = mybir.dt.uint8
U32 = mybir.dt.uint32
ALU = mybir.AluOpType
ACT = mybir.ActivationFunctionType
AX = mybir.AxisListType

P = 128
D = 256
KD = D // P
H = 16
HD = D // H
NQ = 1024
QT = NQ // P
NK = 6404
KC = 512
NKC = NK // KC
TAIL = NK - NKC * KC
TAILW = TAIL // 4
VT = 4 * (NKC + 1)
PARTS = 3
QR = PARTS * HD
RG = H * QR // P
SC = 1024
FIRST = (NK - KC) % SC
SCS = [(0, FIRST)] + [(a, SC) for a in range(FIRST, NK - KC, SC)] + [(NK - KC, KC)]
NSC = len(SCS)
UNITS = H * QT
STEPS = UNITS // 2
WG = 4
E = 64
I = 64
EG = 4
NEG = E // EG
TOPK = 8
ROUND = 1.5 * 2.0 ** 23
LN255 = 5.541263545158426
LN_EPS = 1e-5
QMIN = 1e-8


def last_axis(ap, n):
    return ap.unsqueeze(len(ap.shape)).broadcast_to(list(ap.shape) + [n])


def middle_axis(ap, n):
    return ap.unsqueeze(1).broadcast_to([ap.shape[0], n, ap.shape[1]])


def product(nc, out, stationary, moving, start, stop, **kw):
    (a_hi, a_lo), (b_hi, b_lo) = stationary, moving
    nc.tensor.matmul(out, a_hi, b_hi, start=start, stop=False, **kw)
    nc.tensor.matmul(out, a_hi, b_lo, start=False, stop=False, **kw)
    return nc.tensor.matmul(out, a_lo, b_hi, start=False, stop=stop, **kw)


class Steps:

    def __init__(self, engine, sem, base=0):
        self.engine, self.sem, self.n, self.base = engine, sem, 0, base

    def then(self, instruction):
        instruction.then_inc(self.sem, 1)
        self.n += 1
        self.engine.wait_ge(self.sem, self.base + self.n)


LN_STEPS = 8
VAR_STEP = 3


def layernorm(nc, dve, steps, x, stats, mv, ln, out, root, ready, tiles, n):
    first = steps.n
    ts = slice(tiles[0], tiles[-1] + 1)
    for t in tiles:
        done = nc.vector.bn_stats(stats[:, t, :], x[:, t, :])
    steps.then(done)
    for t in tiles:
        done = nc.vector.bn_aggr(mv[:, t, :], stats[:, t, :])
    steps.then(done)
    steps.then(nc.vector.tensor_scalar(ln[:, 0, ts], mv[:, ts, 1], LN_EPS, None, ALU.add))
    assert steps.n == first + VAR_STEP
    dve.wait_ge(root, n)
    steps.then(nc.vector.reciprocal(ln[:, 2, ts], ln[:, 1, ts]))
    steps.then(nc.vector.tensor_tensor(ln[:, 3, ts], ln[:, 0, ts], ln[:, 2, ts], ALU.mult))
    steps.then(nc.vector.tensor_tensor(ln[:, 3, ts], ln[:, 3, ts], ln[:, 2, ts], ALU.mult))
    steps.then(nc.vector.tensor_scalar(ln[:, 3, ts], ln[:, 3, ts], -0.5, 1.5, ALU.mult, ALU.add))
    steps.then(nc.vector.tensor_tensor(ln[:, 2, ts], ln[:, 2, ts], ln[:, 3, ts], ALU.mult))
    for t in tiles:
        done = nc.vector.tensor_scalar(out[:, t, :], x[:, t, :], mv[:, t, 0:1], ln[:, 2, t:t + 1],
                                       ALU.subtract, ALU.mult)
    done.then_inc(ready, 1)
    dve.wait_ge(ready, n)
    assert steps.n == first + LN_STEPS


def projections(nc, io, keep, scratch):
    x, ident, sv, sq, v, kT, qT, heads_in = (keep[n] for n in ("x", "ident", "sv", "sq", "v", "kT", "qT", "heads_in"))
    kT_d, qT_d = scratch
    with ExitStack() as ctx:
        def sb(name, shape, dt=F32):
            return ctx.enter_context(nc.sbuf_tensor(name, shape, dt))

        def psum(name, shape, dt=F32):
            return ctx.enter_context(nc.psum_tensor(name, shape, dt))

        def sem(name):
            return ctx.enter_context(nc.semaphore(name))

        NC = NKC + 1
        ITEMS = NC + 2
        VP = 4 * KC
        VPS = [(a, min(VP, NK - a)) for a in range(0, NK, VP)]
        identb = sb("identb", [P, P], BF16)
        wq = sb("wq", [P, KD, D])
        wkv = sb("wkv", [P, KD, 2 * D])
        bq = sb("bq", [P, D])
        bk = sb("bk", [P, D])
        bv = sb("bv", [P, KD])
        stats = sb("stats", [P, QT, 6])
        mv = sb("mv", [P, QT, 2])
        ln = sb("ln", [P, 4, QT])
        h = keep["o"][:, :].rearrange("p (t d) -> p t d", t=QT)
        hT = sb("hT", [P, KD, NQ])
        qmax = sb("qmax", [P, QT * H])
        qscale = sb("qscale", [P, QT * H])
        qinv = sb("qinv", [P, QT * H])
        ctxc = sb("ctxc", [P, 2, KD, KC])
        kf = sb("kf", [P, 4, D])
        kr = sb("kr", [P, 4, D])
        kq = sb("kq", [P, 2, 4, D])
        kres = sb("kres", [P, 4, D])
        amax = sb("amax", [P, 4 * H])
        kscale = sb("kscale", [P, 4 * H])
        kinv = sb("kinv", [P, 4 * H])
        parts = sb("parts", [P, 2, 4, H, QR], BF16)
        turned = sb("turned", [P, 2, RG, KC], BF16)
        vT = sb("vT", [P, KD, NK])
        vm = sb("vm", [P, KD, NC])
        vcol = sb("vcol", [P, KD])
        vinv = sb("vinv", [P, KD])
        vint = [t.bitcast(BF16).rearrange("p (k n) -> p k n", k=KD)
                for t in (hT[:, :, :].rearrange("p k n -> p (k n)"), keep["o"][:, :])]

        pk = psum("pk", [P, 4, D])
        pv = psum("pv", [P, KD, KC])
        pt = psum("pt", [P, 8, KC], BF16)
        vbank = [t.rearrange("p a b -> p (a b)")[:, n * KC:(n + 1) * KC].bitcast(BF16)
                 for t in (pk[:, :, :], pv[:, :, :]) for n in range(2)]
        ptf = pt[:, :, :].rearrange("p a b -> p (a b)").bitcast(F32)

        x_in = sem("x_in")
        loaded = sem("loaded")
        w_loaded = sem("w_loaded")
        wq_loaded = sem("wq_loaded")
        ctx_in = [sem("ctx_in0"), sem("ctx_in1")]
        consts = sem("consts")
        qsteps = sem("qsteps")
        identb_ready = sem("identb_ready")
        root = sem("root")
        h_ready = sem("h_ready")
        hT_turned = sem("hT_turned")
        hT_ready = sem("hT_ready")
        q_ready = sem("q_ready")
        q_taken = sem("q_taken")
        qparts = sem("qparts")
        k_ready = sem("k_ready")
        v_ready = sem("v_ready")
        ksteps = sem("ksteps")
        k_taken = sem("k_taken")
        kq_ready = sem("kq_ready")
        v_taken = sem("v_taken")
        v_max = sem("v_max")
        hi_done = sem("hi_done")
        res_done = sem("res_done")
        mid_done = sem("mid_done")
        kparts = sem("kparts")
        turned_ready = sem("turned_ready")
        turned_taken = sem("turned_taken")
        stored = [sem("stored0"), sem("stored1")]
        vsteps = sem("vsteps")
        v_shifted = sem("v_shifted")
        v_shifted2 = sem("v_shifted2")
        v_rounded = sem("v_rounded")
        v_rounded2 = sem("v_rounded2")
        v_turned = sem("v_turned")
        v_kept = [sem("v_kept0"), sem("v_kept1")]

        block = ctx.enter_context(nc.Block())
        LK = 5
        ctx_view = io["ctxT"].rearrange("(k p) n -> p k n", p=P)

        @block.sync
        def _(sp):
            def load(c, par, width):
                sp.dma_start(ctxc[:, par, :, 0:width],
                             ctx_view[:, :, bass.ds(c * KC, width)]).then_inc(ctx_in[par], 16)

            def store(n, par, dram, at, width):
                sp.wait_ge(turned_taken, n + 1)
                dst = dram.rearrange("h r n -> (h r) n").rearrange("(g p) n -> p g n", p=P)
                sp.dma_start(dst[:, :, bass.ds(at, width)],
                             turned[:, par, :, 0:width]).then_inc(stored[par], 16)

            sp.dma_start(x[:, :, :], io["x"].rearrange("(t p) d -> p t d", p=P)).then_inc(x_in, 16)
            sp.dma_start(wkv[:, :, :], io["Wkv"].rearrange("(k p) n -> p k n", p=P)).then_inc(w_loaded, 16)
            load(0, 0, KC)
            sp.dma_start(ident[:, :], io["eye"]).then_inc(loaded, 16)
            sp.dma_start(bk[:, :], io["bkv"][:, 0:D].broadcast_to([P, D])).then_inc(w_loaded, 16)
            sp.dma_start(bv[:, :], io["bv"]).then_inc(w_loaded, 16)
            sp.dma_start(wq[:, :, :], io["Wq"].rearrange("(k p) n -> p k n", p=P)).then_inc(wq_loaded, 16)
            load(1, 1, KC)
            sp.dma_start(bq[:, :], io["bq"].broadcast_to([P, D])).then_inc(loaded, 16)
            for c in range(2):
                sp.wait_ge(v_ready, c + 1)
                load(c + 2, c, KC)
            for c in range(2):
                store(c, c, kT_d, c * KC, KC)
            for n in range(2, 4):
                store(n, n % 2, qT_d, (n - 2) * KC, KC)
                sp.wait_ge(v_ready, n + 1)
                load(n + 2, n % 2, KC)
            with sp.Fori(2, NKC // 2 - 1) as i:
                for par in range(2):
                    n = 2 * i + par
                    store(n, par, kT_d, (n - 2) * KC, KC)
                    sp.wait_ge(v_ready, n + 1)
                    load(n + 2, par, KC)
            store(NKC - 2, 0, kT_d, (NKC - 4) * KC, KC)
            sp.wait_ge(v_ready, NKC - 1)
            load(NKC, 0, TAIL)
            for n in range(NKC - 1, ITEMS):
                store(n, n % 2, kT_d, (n - 2) * KC, KC if n < ITEMS - 1 else TAIL)
            sp.wait_ge(stored[0], 16 * (NKC // 2 + 2))
            sp.wait_ge(stored[1], 16 * (NKC // 2 + 1))
            sp.wait_ge(consts, 3)
            for head in range(2):
                sp.dma_start(kT[0:QR, head, :], kT_d[head]).then_inc(heads_in[head], 16)
                sp.dma_start(qT[0:QR, head, :], qT_d[head, :, 0:2 * P]).then_inc(heads_in[head], 16)

        @block.gpsimd
        def _(pool):
            pool.memset(v[:, :, VT - 4:VT, :], 0.0).then_inc(consts, 1)
            pool.memset(kT[:, :, :].rearrange("p a n -> p (a n)").bitcast(U32), 0).then_inc(consts, 1)
            pool.memset(qT[:, :, :].rearrange("p a n -> p (a n)").bitcast(U32), 0).then_inc(consts, 1)

            def residuals(c, par):
                pool.wait_ge(hi_done, c + 1)
                if not (isinstance(c, int) and c == 0):
                    pool.wait_ge(kparts, c)
                pool.tensor_tensor(kres[:, :, :].rearrange("p i (h e) -> p i h e", h=H),
                                   kq[:, par].rearrange("p i (h e) -> p i h e", h=H),
                                   parts[:, par, :, :, 0:HD], ALU.subtract).then_inc(res_done, 1)
                pool.wait_ge(mid_done, c + 1)
                pool.tensor_tensor(parts[:, par, :, :, 2 * HD:3 * HD],
                                   kres[:, :, :].rearrange("p i (h e) -> p i h e", h=H),
                                   parts[:, par, :, :, HD:2 * HD], ALU.subtract).then_inc(kparts, 1)

            residuals(0, 0)
            residuals(1, 1)
            with pool.Fori(1, NKC // 2) as i:
                for par in range(2):
                    residuals(2 * i + par, par)
            residuals(NKC, 0)
            for n, (a, w) in enumerate(VPS):
                if n == 0:
                    pool.wait_ge(v_shifted, 1)
                else:
                    pool.wait_ge(vsteps, 3)
                    pool.tensor_scalar(vT[:, 1, a:a + w], vT[:, 1, a:a + w], vinv[:, 1:2], ROUND,
                                       ALU.mult, ALU.add).then_inc(v_shifted2, 1)
                    pool.wait_ge(v_shifted2, n)
                if n >= 2:
                    pool.wait_ge(v_turned, 4 * (n - 1))
                pool.tensor_scalar(vint[n % 2][:, 1, 0:w], vT[:, 1, a:a + w], -ROUND, 1.0,
                                   ALU.add, ALU.mult).then_inc(v_rounded2, 1)

        def keep_tile(t):
            m = min(P, NK // 4 - t * P)
            return (v[0:m, :, 4 * t:4 * t + 4, :].rearrange("p h b e -> p b h e"),
                    vbank[t % 4][0:m, :].rearrange("p (b h e) -> p b h e", b=4, h=H))

        @block.scalar
        def _(act):
            act.wait_ge(qsteps, VAR_STEP)
            nc.scalar.activation(ln[:, 1, :], ln[:, 0, :], ACT.Sqrt).then_inc(root, 1)
            for k in range(KD):
                act.wait_ge(hT_turned, k + 1)
                nc.scalar.copy(hT[:, k, :], ptf[:, k * NQ:(k + 1) * NQ]).then_inc(hT_ready, 1)

            def chunk(c, par, width=KC):
                act.wait_ge(kq_ready, c + 1)
                if not (isinstance(c, int) and c < 2):
                    act.wait_ge(turned_ready, c + 1)
                nc.scalar.copy(parts[:, par, :, :, 0:HD],
                               kq[:, par].rearrange("p i (h e) -> p i h e", h=H)).then_inc(hi_done, 1)
                act.wait_ge(v_ready, c + 1)
                for k in range(KD):
                    done = nc.scalar.activation(vT[:, k, bass.ds(c * KC, width)], pv[:, k, 0:width], ACT.Identity,
                                                bias=bv[:, k:k + 1])
                done.then_inc(v_taken, 1)
                act.wait_ge(res_done, c + 1)
                nc.scalar.copy(parts[:, par, :, :, HD:2 * HD],
                               kres[:, :, :].rearrange("p i (h e) -> p i h e", h=H)).then_inc(mid_done, 1)

            def evacuate_item(n, par, uses, width=KC):
                act.wait_ge(turned_ready, n + 1)
                if not (isinstance(uses, int) and uses == 0):
                    act.wait_ge(stored[par], 16 * uses)
                nc.scalar.copy(turned[:, par, :, 0:width], pt[:, 0:RG, 0:width]).then_inc(turned_taken, 1)

            act.wait_ge(w_loaded, 48)
            act.wait_ge(consts, 1)
            chunk(0, 0)
            chunk(1, 1)
            for n in range(3):
                evacuate_item(n, n % 2, n // 2)
            with act.Fori(1, NKC // 2) as i:
                chunk(2 * i, 0)
                evacuate_item(2 * i + 1, 1, i)
                chunk(2 * i + 1, 1)
                evacuate_item(2 * i + 2, 0, i + 1)
            chunk(NKC, 0, TAIL)
            evacuate_item(NKC + 1, 1, NKC // 2)
            evacuate_item(NKC + 2, 0, NKC // 2 + 1, TAIL)
            for t in range(0, NC, 2):
                act.wait_ge(v_turned, t + 1)
                nc.scalar.copy(*keep_tile(t)).then_inc(v_kept[0], 1)

        @block.tensor
        def _(pe):
            def project_k(c, par, width, loads):
                pe.wait_ge(ctx_in[par], 16 * loads)
                if not (isinstance(c, int) and c == 0):
                    pe.wait_ge(k_taken, c)
                for i in range(-(-width // P)):
                    m = min(P, width - i * P)
                    for k in range(KD):
                        mm = nc.tensor.matmul(pk[0:m, i, :], ctxc[:, par, k, i * P:i * P + m], wkv[:, k, 0:D],
                                              start=(k == 0), stop=(k == KD - 1))
                mm.then_inc(k_ready, 1)

            def project_v(c, par, width):
                if not (isinstance(c, int) and c == 0):
                    pe.wait_ge(v_taken, c)
                for n in range(KD):
                    for k in range(KD):
                        mm = nc.tensor.matmul(pv[:, n, 0:width], wkv[:, k, D + n * P:D + (n + 1) * P],
                                              ctxc[:, par, k, 0:width], start=(k == 0), stop=(k == KD - 1))
                mm.then_inc(v_ready, 1)

            def turn(n, par, width=KC):
                if isinstance(n, int) and n == 0:
                    pe.wait_ge(q_taken, 1)
                else:
                    pe.wait_ge(turned_taken, n)
                if isinstance(n, int) and n < 4:
                    pe.wait_ge(kparts if n < 2 else qparts, n % 2 + 1)
                else:
                    pe.wait_ge(kparts, n - 1)
                for i in range(-(-width // P)):
                    for g in range(RG):
                        mm = nc.tensor.transpose(
                            pt[:, g, i * P:(i + 1) * P],
                            parts[:, par, i].rearrange("p h r -> p (h r)")[:, g * P:(g + 1) * P], identb[:, :])
                mm.then_inc(turned_ready, 1)

            pe.wait_ge(w_loaded, 48)
            project_k(0, 0, KC, 1)
            project_v(0, 0, KC)
            pe.wait_ge(h_ready, 1)
            pe.wait_ge(loaded, 16 * 2)
            for k in range(KD):
                for t in range(QT):
                    mm = nc.tensor.transpose(ptf[:, k * NQ + t * P:k * NQ + (t + 1) * P],
                                             h[:, t, k * P:(k + 1) * P], ident[:, :])
                mm.then_inc(hT_turned, 1)
            project_k(1, 1, KC, 1)
            pe.wait_ge(hT_ready, KD)
            pe.wait_ge(wq_loaded, 16)
            for t in range(QT):
                for k in range(KD):
                    mm = nc.tensor.matmul(ptf[:, t * D:(t + 1) * D], hT[:, k, t * P:(t + 1) * P], wq[:, k, :],
                                          start=(k == 0), stop=(k == KD - 1))
            mm.then_inc(q_ready, 1)
            project_v(1, 1, KC)
            pe.wait_ge(identb_ready, 1)
            turn(0, 0)
            project_k(2, 0, KC, 2)
            turn(1, 1)
            project_v(2, 0, KC)
            turn(2, 0)
            project_k(3, 1, KC, 2)
            turn(3, 1)
            project_v(3, 1, KC)
            with pe.Fori(2, NKC // 2) as i:
                for par in range(2):
                    project_k(2 * i + par, par, KC, i + 1)
                    turn(2 * i + par, par)
                    project_v(2 * i + par, par, KC)
            project_k(NKC, 0, TAIL, NKC // 2 + 1)
            turn(NKC, 0)
            project_v(NKC, 0, TAIL)
            turn(NKC + 1, 1)
            turn(NKC + 2, 0, TAIL)

            pe.wait_ge(k_taken, NC)
            pe.wait_ge(v_taken, NC)
            for t in range(NC):
                n = t // 4
                m = min(P, NK // 4 - t * P)
                if t % 4 == 0:
                    pe.wait_ge(v_rounded, n + 1)
                    pe.wait_ge(v_rounded2, n + 1)
                if t >= 4:
                    pe.wait_ge(v_kept[t % 2], t // 2 - 1)
                for b in range(4):
                    for k in range(KD):
                        a = (t % 4) * 4 * P + b
                        mm = nc.tensor.transpose(vbank[t % 4][0:m, b * D + k * P:][:, 0:P],
                                                 vint[n % 2][:, k, a:a + 4 * m - 3:4], identb[:, :])
                mm.then_inc(v_turned, 1)

        @block.vector
        def _(dve):
            q = Steps(dve, qsteps)
            dve.wait_ge(x_in, 16)
            layernorm(nc, dve, q, x, stats, mv, ln, h, root, h_ready, range(QT), 1)

            def heads(t):
                return t.rearrange("p i (h e) -> p (i h) e", e=HD)

            def quantise(c, par):
                k = Steps(dve, ksteps, LK * c)
                dve.wait_ge(k_ready, c + 1)
                nc.vector.tensor_tensor(kf[:, :, :], pk[:, :, :], middle_axis(bk[:, :], 4),
                                        ALU.add).then_inc(k_taken, 1)
                dve.wait_ge(k_taken, c + 1)
                k.then(nc.vector.tensor_reduce(amax[:, :], heads(kf[:, :, :]), AX.X, ALU.max,
                                               apply_absolute_value=True))
                k.then(nc.vector.tensor_scalar(kscale[:, :], amax[:, :], 1.0 / 127.0, QMIN, ALU.mult, ALU.max))
                k.then(nc.vector.reciprocal(kinv[:, :], kscale[:, :]))
                k.then(nc.vector.tensor_tensor(heads(kr[:, :, :]), heads(kf[:, :, :]), last_axis(kinv[:, :], HD),
                                               ALU.mult))
                k.then(nc.vector.tensor_scalar(kr[:, :, :], kr[:, :, :], ROUND, ROUND, ALU.add, ALU.subtract))
                if not (isinstance(c, int) and c < 2):
                    dve.wait_ge(res_done, c - 1)
                nc.vector.tensor_tensor(heads(kq[:, par]), heads(kr[:, :, :]), last_axis(kscale[:, :], HD),
                                        ALU.mult).then_inc(kq_ready, 1)

            def v_maxima(c, width=KC):
                dve.wait_ge(v_taken, c + 1)
                nc.vector.tensor_reduce(vm[:, :, bass.ds(c, 1)].rearrange("p k o -> p (k o)"),
                                        vT[:, :, bass.ds(c * KC, width)], AX.X, ALU.max,
                                        apply_absolute_value=True).then_inc(v_max, 1)

            dve.wait_ge(loaded, 16 * 2)
            nc.vector.tensor_copy(identb[:, :], ident[:, :]).then_inc(identb_ready, 1)
            dve.wait_ge(w_loaded, 48)
            quantise(0, 0)
            quantise(1, 1)
            dve.wait_ge(q_ready, 1)
            nc.vector.tensor_tensor(h, ptf.rearrange("p (t d) -> p t d", t=QT), middle_axis(bq[:, :], QT),
                                    ALU.add).then_inc(q_taken, 1)
            dve.wait_ge(q_taken, 1)
            q.then(nc.vector.tensor_reduce(qmax[:, :], heads(h), AX.X, ALU.max, apply_absolute_value=True))
            q.then(nc.vector.tensor_scalar(qscale[:, :], qmax[:, :], 1.0 / 127.0, 4 * QMIN, ALU.mult, ALU.max))
            q.then(nc.vector.reciprocal(qinv[:, :], qscale[:, :]))
            nc.vector.tensor_scalar(sq[:, :, :].rearrange("p (g h) j -> p g h j", h=H),
                                    qscale[:, :].rearrange("p (g j h) -> p g h j", g=QT // 2, j=2),
                                    0.25, None, ALU.mult)
            q.then(nc.vector.tensor_tensor(heads(h), heads(h), last_axis(qinv[:, :], HD), ALU.mult))
            for r in range(2):
                dve.wait_ge(turned_ready, r + 1)
                for part in range(PARTS):
                    done = nc.vector.tensor_scalar(
                        parts[:, r, :, :, part * HD:(part + 1) * HD].rearrange("p i h e -> p (i h) e"),
                        heads(h[:, 4 * r:4 * r + 4, :]), ROUND, ROUND, ALU.add, ALU.subtract)
                done.then_inc(qparts, 1)
            v_maxima(0)
            with dve.Fori(1, NKC // 2) as i:
                for par in range(2):
                    quantise(2 * i + par, par)
                    v_maxima(2 * i + par - 1)
            quantise(NKC, 0)
            v_maxima(NKC - 1)
            v_maxima(NKC, TAIL)

            s = Steps(dve, vsteps)
            dve.wait_ge(v_max, NC)
            s.then(nc.vector.tensor_reduce(vcol[:, :], vm[:, :, :], AX.X, ALU.max))
            s.then(nc.vector.tensor_scalar(sv[:, :], vcol[:, :], 1.0 / 127.0, QMIN, ALU.mult, ALU.max))
            s.then(nc.vector.reciprocal(vinv[:, :], sv[:, :]))
            for n, (a, w) in enumerate(VPS):
                for k in (1, 0) if n == 0 else (0,):
                    done = nc.vector.tensor_scalar(vT[:, k, a:a + w], vT[:, k, a:a + w], vinv[:, k:k + 1], ROUND,
                                                   ALU.mult, ALU.add)
                done.then_inc(v_shifted, 1)
                dve.wait_ge(v_shifted, n + 1)
                if n >= 2:
                    dve.wait_ge(v_turned, 4 * (n - 1))
                nc.vector.tensor_scalar(vint[n % 2][:, 0, 0:w], vT[:, 0, a:a + w], ROUND, None,
                                        ALU.subtract).then_inc(v_rounded, 1)
                for t in range(4 * n - 3, 4 * n, 2):
                    if t >= 0:
                        dve.wait_ge(v_turned, t + 1)
                        nc.vector.tensor_copy(*keep_tile(t)).then_inc(v_kept[1], 1)


def over_sums(nc, keep, tiles):
    rs = keep["rsum"][:, :].rearrange("p (g h j) -> p g j h", h=H, j=2)
    ov = keep["o"][:, :].rearrange("p (g h j d) -> p g j h d", h=H, j=2, d=HD)
    for t in tiles:
        done = nc.vector.tensor_tensor(keep["on"][:, t, :].rearrange("p (h d) -> p h d", h=H), ov[:, t // 2, t % 2],
                                       last_axis(rs[:, t // 2, t % 2], HD), ALU.mult)
    return done


def attention(nc, io, keep, scratch):
    ident, sq, o, sums, v = (keep[n] for n in ("ident", "sq", "o", "sums", "v"))
    kT, qT, heads_in = (keep[n] for n in ("kT", "qT", "heads_in"))
    kT_d, qT_d = scratch
    LOOP = 16
    ORDER = [WG - 1] + list(range(WG - 1))
    LAG_T, LAG_PV = 2, 3
    with ExitStack() as ctx:
        def sb(name, shape, dt=F32):
            return ctx.enter_context(nc.sbuf_tensor(name, shape, dt))

        def psum(name, shape, dt=F32):
            return ctx.enter_context(nc.psum_tensor(name, shape, dt))

        def sem(name):
            return ctx.enter_context(nc.semaphore(name))

        vh = sb("vh", [P, 2, VT, HD], BF16)
        s = sb("s", [P, 2, NK])
        e8 = sb("e8", [P, 2, NK], U8)
        words = sb("words", [P, 2, NKC + 1, P], U32)
        pT = sb("pT", [P, 2, VT, P], BF16)
        smax = sb("smax", [P, 2, NSC])
        nmax = sb("nmax", [P, 2])
        bias = sb("bias", [P, 2])

        ps = psum("ps", [P, 2, SC])
        pw = psum("pw", [P, 3, KC])
        po = psum("po", [P, KC])

        v_in = [sem("v_in0"), sem("v_in1")]
        scored = sem("scored")
        copied = sem("copied")
        max_ready = sem("max_ready")
        bias_ready = sem("bias_ready")
        exped = sem("exped")
        turned = sem("turned")
        wordsd = sem("wordsd")
        unpacked = sem("unpacked")
        weighed = sem("weighed")
        o_taken = sem("o_taken")
        last_unpacked = sem("last_unpacked")
        rows_done = sem("rows_done")
        pool_passed = sem("pool_passed")

        sqf = sq[:, :, :].rearrange("p s j -> p (s j)")

        def unpacking(j, g):
            m, a, b = (P, 4 * g, 4 * g + 4) if g < WG - 1 else (TAILW, NKC, NKC + 1)
            return (pT[0:m, j, 4 * a:4 * b, :].rearrange("p (t b) q -> p t b q", b=4),
                    words[0:m, j, a:b, :].bitcast(U8).rearrange("p t (q b) -> p t b q", b=4))

        block = ctx.enter_context(nc.Block())

        def first(n):
            return isinstance(n, int) and n < 2

        @block.sync
        def _(sp):
            def load_heads(st, par, head, group):
                if not first(st):
                    sp.wait_ge(scored, 2 * NSC * (st - 1))
                sp.dma_start(kT[0:QR, par, :],
                             kT_d[bass.ds(head, 1)].rearrange("o r n -> (o r) n")).then_inc(heads_in[par], 16)
                sp.dma_start(qT[0:QR, par, :],
                             qT_d[bass.ds(head, 1), :, bass.ds(group * 2 * P, 2 * P)]
                             .rearrange("o r n -> (o r) n")).then_inc(heads_in[par], 16)

            def load_v(st, par, head):
                if not first(st):
                    sp.wait_ge(weighed, 2 * (st - 1))
                sp.dma_start(vh[:, par].rearrange("p t d -> p (t d)"),
                             v[:, bass.ds(head, 1)].rearrange("p o t d -> p (o t d)")).then_inc(v_in[par], 16)

            load_v(0, 0, 0)
            load_heads(2, 0, 2, 0)
            load_v(1, 1, 1)
            load_heads(3, 1, 3, 0)
            load_v(2, 0, 2)
            for dst, src in ((keep["wp"][:, :, :], io["Wp"].rearrange("(k p) n -> p k n", p=P)),
                             (keep["bp"][:, :], io["bp"].broadcast_to([P, D])),
                             (keep["gates"][:, 0:1], io["g_xattn"].broadcast_to([P, 1])),
                             (keep["gates"][:, 1:2], io["g_ffn"].broadcast_to([P, 1])),
                             (keep["router"][:, :, :], io["router"].rearrange("(k p) n -> p k n", p=P))):
                sp.dma_start(dst, src).then_inc(keep["ffn_loaded"], 16)
            with sp.Fori(2, STEPS // 2) as i:
                group, hp = i // (H // 2), i % (H // 2)
                load_heads(2 * i, 0, 2 * hp, group)
                load_v(2 * i - 1, 1, (2 * hp + H - 1) % H)
                load_heads(2 * i + 1, 1, 2 * hp + 1, group)
                load_v(2 * i, 0, 2 * hp)
            load_v(STEPS - 1, 1, H - 1)
            for par in range(2):
                sp.wait_ge(heads_in[par], 32 * (STEPS // 2))
                sp.wait_ge(v_in[par], 16 * (STEPS // 2))

        @block.tensor
        def _(pe):
            def scores(u, par, j, early, c):
                a, w = SCS[c]
                n = NSC * u + c
                if not (early and u == 0 and c < 2):
                    pe.wait_ge(copied, n - 1)
                if c == 1 and not (early and u < LAG_T + 1):
                    pe.wait_ge(wordsd, WG * (u - LAG_T - 1) + 1)
                for b in range(a, a + w, KC):
                    m = min(KC, a + w - b)
                    mm = nc.tensor.matmul(ps[:, buffer(j, c), b - a:b - a + m], qT[:, par, j * P:(j + 1) * P],
                                          kT[:, par, b:b + m], start=True, stop=True)
                mm.then_inc(scored, 1)

            def buffer(j, c):
                return (NSC * j + c) % 2

            def turn(w_, j, g, early):
                if g == 0:
                    pe.wait_ge(exped, w_ + 1)
                if g < WG - 1:
                    if not early:
                        pe.wait_ge(wordsd, WG * (w_ - 1) + g + 2)
                    out = pw[:, g, :]
                else:
                    out = ps[:, buffer(j, NSC - 1), KC:2 * KC]
                ew = e8[:, j, :].bitcast(F32)
                for t in range(4 * g, min(4 * g + 4, NKC + 1)):
                    m = min(P, NK // 4 - t * P)
                    mm = nc.tensor.transpose(out[0:m, (t % 4) * P:(t % 4 + 1) * P], ew[:, t * P:t * P + m],
                                             ident[:, :])
                mm.then_inc(turned, 1)

            def weigh(w_, k, loads, n, early):
                par, j = k // 2, k % 2
                g = ORDER[n]
                if n == 0:
                    pe.wait_ge(v_in[par], 16 * loads)
                    if j == 0 and not (early and w_ == 0):
                        pe.wait_ge(o_taken, w_ // 2)
                if isinstance(w_, int) and w_ == UNITS - 1:
                    pe.wait_ge(last_unpacked, n + 1)
                else:
                    pe.wait_ge(unpacked, WG * w_ + n + 1)
                for t in range(16 * g, min(16 * g + 16, VT)):
                    m = min(P, NK // 4 - (t // 4) * P)
                    mm = nc.tensor.matmul(po[:, j * HD:(j + 1) * HD], pT[0:m, j, t, :], vh[0:m, par, t, :],
                                          start=(t == 16 * ORDER[0]), stop=(t == 16 * ORDER[-1] + 15))
                if n == WG - 1:
                    mm.then_inc(weighed, 1)

            def unit(i, k, early=False):
                u, par, j = 4 * i + k, k // 2, k % 2
                turns = not early or u >= LAG_T
                weighs = not early or u >= LAG_PV
                kv = (k - LAG_PV) % 4
                loads = i + 1 if k >= LAG_PV else i
                if j == 0:
                    pe.wait_ge(heads_in[par], 32 * (i + 1))
                for c in range(NSC):
                    scores(u, par, j, early, c)
                    if turns and 1 <= c < WG:
                        turn(u - LAG_T, j, c - 1, early and u == LAG_T)
                    if turns and c == NSC - 1:
                        turn(u - LAG_T, j, WG - 1, early)
                    if weighs and c == 4:
                        weigh(u - LAG_PV, kv, loads, 0, early)
                    if weighs and c >= 4:
                        weigh(u - LAG_PV, kv, loads, c - 3, early)

            for k in range(4):
                unit(0, k, True)
            with pe.Fori(1, UNITS // 4) as i:
                for k in range(4):
                    unit(i, k)
            pe.wait_ge(copied, NSC * UNITS)
            for u in range(UNITS, UNITS + LAG_PV):
                if u < UNITS + LAG_T:
                    for g in range(WG):
                        if g == WG - 1 and u > UNITS:
                            pe.wait_ge(wordsd, WG * (u - LAG_T - 1) + 1)
                        turn(u - LAG_T, u % 2, g, False)
                w_ = u - LAG_PV
                for n in range(WG):
                    weigh(w_, w_ % 4, w_ // 4 + 1, n, False)

        @block.scalar
        def _(act):
            def exp(u, j, early):
                act.wait_ge(bias_ready, u + 1)
                if not early:
                    act.wait_ge(turned, WG * (u - 1))
                nc.scalar.activation(e8[:, j, :], s[:, j, :], ACT.Exp, bias=bias[:, j:j + 1],
                                     scale=sqf[:, bass.ds(u, 1)], accum_out=sums[:, bass.ds(u, 1)]).then_inc(exped, 1)

            def take_words(w_, j, early):
                if not early:
                    act.wait_ge(unpacked, WG * (w_ - 1))
                act.wait_ge(turned, WG * (w_ + 1))
                for g in ORDER:
                    if g < WG - 1:
                        nc.scalar.copy(words[:, j, 4 * g:4 * g + 4, :].rearrange("p t q -> p (t q)"),
                                       pw[:, g, :].bitcast(U32)).then_inc(wordsd, 1)
                    else:
                        nc.scalar.copy(words[0:TAILW, j, NKC, :],
                                       ps[0:TAILW, (NSC * j + NSC - 1) % 2, KC:KC + P].bitcast(U32)).then_inc(wordsd, 1)

            exp(0, 0, True)
            exp(1, 1, True)
            take_words(0, 0, True)
            exp(2, 0, False)
            take_words(1, 1, True)
            exp(3, 1, False)
            for u in range(4, LOOP):
                take_words(u - 2, u % 2, False)
                exp(u, u % 2, False)
            with act.Fori(1, UNITS // LOOP) as i:
                for k in range(LOOP):
                    take_words(LOOP * i + k - 2, k % 2, False)
                    exp(LOOP * i + k, k % 2, False)
            for j in range(2):
                take_words(UNITS - 2 + j, j, False)

        @block.gpsimd
        def _(pool):
            def unpack(w_, j, early):
                if not early:
                    pool.wait_ge(weighed, w_ - 1)
                for n, g in enumerate(ORDER):
                    pool.wait_ge(wordsd, WG * w_ + n + 1)
                    pool.sem_inc(pool_passed, 1)
                    nc.gpsimd.tensor_scalar(*unpacking(j, g), 1.0, 0.0, ALU.mult, ALU.add).then_inc(unpacked, 1)

            for w_ in range(LOOP):
                unpack(w_, w_ % 2, w_ < 2)
            with pool.Fori(1, UNITS // LOOP - 1) as i:
                for k in range(LOOP):
                    unpack(LOOP * i + k, k % 2, False)
            for w_ in range(UNITS - LOOP, UNITS - 1):
                unpack(w_, w_ % 2, False)

        @block.vector
        def _(dve):
            def take_o(pair):
                dve.wait_ge(weighed, 2 * pair + 2)
                nc.vector.tensor_copy(o[:, bass.ds(pair * 2 * HD, 2 * HD)], po[:, 0:2 * HD]).then_inc(o_taken, 1)

            def maximum(u, j):
                dve.wait_ge(copied, NSC * (u + 1))
                nc.vector.tensor_reduce(nmax[:, j:j + 1], smax[:, j, :], AX.X, ALU.max,
                                        negate=True).then_inc(max_ready, 1)

            def make_bias(u, j):
                dve.wait_ge(max_ready, u + 1)
                nc.vector.tensor_scalar(bias[:, j:j + 1], nmax[:, j:j + 1], sqf[:, bass.ds(u, 1)], LN255,
                                        ALU.mult, ALU.add).then_inc(bias_ready, 1)

            def unit(u, j, early=False):
                if not (early and u < 2):
                    dve.wait_ge(exped, u - 1)
                for c, (a, w) in enumerate(SCS):
                    dve.wait_ge(scored, NSC * u + c + 1)
                    nc.vector.tensor_scalar(s[:, j, a:a + w], ps[:, (NSC * j + c) % 2, 0:w], 1.0, None,
                                            ALU.mult, ALU.max, accum_out=smax[:, j, c:c + 1]).then_inc(copied, 1)
                    if c == 0 and not (early and u == 0):
                        make_bias(u - 1, 1 - j)
                if j == 0 and not (early and u < LAG_PV + 1):
                    take_o((u - LAG_PV - 1) // 2)
                maximum(u, j)

            for u in range(LOOP):
                unit(u, u % 2, True)
            with dve.Fori(1, UNITS // LOOP) as i:
                for k in range(LOOP):
                    unit(LOOP * i + k, k % 2, False)
            make_bias(UNITS - 1, 1)
            dve.wait_ge(exped, UNITS - 2 * H)
            dve.wait_ge(o_taken, H * (QT // 2 - 1))
            nc.vector.reciprocal(keep["rsum"][:, 0:UNITS - 2 * H], sums[:, 0:UNITS - 2 * H]).then_inc(rows_done, 1)
            dve.wait_ge(rows_done, 1)
            over_sums(nc, keep, range(QT - 2)).then_inc(rows_done, 1)
            take_o(UNITS // 2 - 2)
            dve.wait_ge(weighed, UNITS - 2)
            for n, g in enumerate(ORDER):
                dve.wait_ge(wordsd, WG * (UNITS - 1) + n + 1)
                nc.vector.tensor_copy(*unpacking(1, g)).then_inc(last_unpacked, 1)
            take_o(UNITS // 2 - 1)


def ffn(nc, io, keep):
    x, ident, sv, sums, rsum, on = (keep[n] for n in ("x", "ident", "sv", "sums", "rsum", "on"))
    wp, bp, gates, router, loaded = (keep[n] for n in ("wp", "bp", "gates", "router", "ffn_loaded"))
    with ExitStack() as ctx:
        def sb(name, shape, dt=F32):
            return ctx.enter_context(nc.sbuf_tensor(name, shape, dt))

        def psum(name, shape, dt=F32):
            return ctx.enter_context(nc.psum_tensor(name, shape, dt))

        def sem(name):
            return ctx.enter_context(nc.semaphore(name))

        bpg = sb("bpg", [P, D])
        zero = sb("zero", [P, 1])
        one = sb("one", [P, 1])
        tgates = sb("tgates", [P, 2])
        wps = sb("wps", [P, KD, D])
        xT = sb("xT", [P, KD, NQ])
        hT_hi = sb("hT_hi", [P, KD, NQ], F32R)
        hT_lo = sb("hT_lo", [P, KD, NQ], F32R)
        y = sb("y", [P, QT, D])
        stats = sb("stats2", [P, QT, 6])
        mv = sb("mv2", [P, QT, 2])
        ln = sb("ln2", [P, 4, QT])
        lmax = sb("lmax", [P, QT])
        probs = sb("probs", [P, QT, E])
        psums = sb("psums", [P, QT])
        top = sb("top", [P, QT, TOPK])
        rest = sb("rest", [P, QT, E])
        sig = sb("sig", [P, QT])
        share = sb("share", [P, QT, E + 1])
        PIECE, WP = 2 * EG * I, KD + 1
        weights = sb("weights", [P, 2, WP, PIECE])
        weights_hi = sb("weights_hi", [P, 2, WP, PIECE], F32R)
        weights_lo = sb("weights_lo", [P, 2, WP, PIECE], F32R)
        th = sb("th", [P, 2, EG * I])
        gl = sb("gl", [P, 2, EG * I])
        gu = sb("gu", [P, 2, EG * I])
        act_in = sb("act_in", [P, 2, EG * I])
        aT_hi = sb("aT_hi", [P, 2, 2 * P], F32R)
        aT_lo = sb("aT_lo", [P, 2, 2 * P], F32R)

        pacc = psum("pacc", [P, QT, D])
        pgu = psum("pgu", [P, 2, 2 * EG * I])
        pat = psum("pat", [P, 2, KC])
        wide = pacc[:, :, :].rearrange("p t d -> p (t d)")

        tanhs = sem("tanhs")
        steps = sem("steps3")
        o_ready = sem("o_ready")
        turned = sem("turned3")
        xT_ready = sem("xT_ready")
        hT_high = sem("hT_high")
        hT_ready = sem("hT_ready3")
        root = sem("root3")
        proj = sem("proj")
        wp_ready = sem("wp_ready")
        h_ready = sem("h_ready3")
        routed = sem("routed")
        shifted = sem("shifted")
        exped = sem("exped3")
        share_ready = sem("share_ready")
        w_in = [sem("w_in0"), sem("w_in1")]
        w_hi = sem("w_hi")
        w_split = sem("w_split")
        gu_ready = sem("gu_ready")
        th_ready = sem("th_ready")
        gl_ready = sem("gl_ready")
        gu_done = sem("gu_done")
        a_ready = sem("a_ready")
        a_turned = sem("a_turned")
        aT_high = sem("aT_high")
        aT_ready = sem("aT_ready")
        added = sem("added")
        xb_ready = sem("xb_ready")
        zero_made = sem("zero_made")
        one_made = sem("one_made")
        zeroed = sem("zeroed")
        y_ready = sem("y_ready")
        out_done = sem("out_done")

        block = ctx.enter_context(nc.Block())
        NU = (NEG + 1) * QT
        LAG_T, LAG_D = 2, 3
        LAST = ((0, QT // 2), (QT // 2, QT))
        HT = QT // 2
        LN_BASE = (2, 2 + LN_STEPS + 1)
        SPLIT_AT = (3, 4, 5)

        @block.sync
        def _(sp):
            def load(g, par):
                sp.dma_start(weights[:, par, 0:KD, :],
                             io["gate_up"][bass.ds(g, 1)].rearrange("o (k p) n -> p (o k) n", p=P)).then_inc(w_in[par], 16)
                sp.dma_start(weights[:, par, KD, :].rearrange("p (k n) -> p k n", k=2),
                             io["down"][bass.ds(g, 1)].rearrange("o (k p) n -> p (o k) n", p=P)).then_inc(w_in[par], 16)

            load(0, 0)
            load(1, 1)
            with sp.Fori(1, NEG // 2) as i:
                for par in range(2):
                    g = 2 * i + par
                    sp.wait_ge(w_split, WP * (g - 1))
                    load(g, par)
            sp.wait_ge(w_split, WP * (NEG - 1))
            sp.dma_start(weights[:, 0, 0:KD, 0:2 * I],
                         io["shared_gate_up"].rearrange("(k p) n -> p k n", p=P)).then_inc(w_in[0], 16)
            sp.dma_start(weights[0:I, 0, KD, 0:D], io["shared_down"]).then_inc(w_in[0], 16)
            out = io["out"].rearrange("(t p) d -> p t d", p=P)
            for n, (a, b) in enumerate(LAST):
                sp.wait_ge(y_ready, n + 1)
                sp.dma_start(out[:, a:b, :], y[:, a:b, :]).then_inc(out_done, 16)
            sp.wait_ge(out_done, 32)

        @block.tensor
        def _(pe):
            def turn_rows(half):
                for k in range(KD):
                    for t in range(HT):
                        mm = nc.tensor.transpose(wide[:, (2 * half + k) * KC + t * P:][:, 0:P],
                                                 on[:, HT * half + t, k * P:(k + 1) * P], ident[:, :])
                    mm.then_inc(turned, 1)

            turn_rows(0)
            pe.wait_ge(o_ready, 1)
            turn_rows(1)
            pe.wait_ge(wp_ready, KD)
            for half in range(2):
                pe.wait_ge(xT_ready, KD * (half + 1))
                for t in range(HT * half, HT * (half + 1)):
                    for k in range(KD):
                        mm = nc.tensor.matmul(pacc[:, t, :], xT[:, k, t * P:(t + 1) * P], wps[:, k, :],
                                              start=(k == 0), stop=(k == KD - 1))
                mm.then_inc(proj, 1)
            for half in range(2):
                pe.wait_ge(h_ready, half + 1)
                turn_rows(half)
                pe.wait_ge(xT_ready, KD * (2 + half + 1))
                for t in range(HT):
                    for k in range(KD):
                        at = (HT * half + t) * P
                        mm = nc.tensor.matmul(pat[:, half, t * P:t * P + E + 1], xT[:, k, at:at + P], router[:, k, :],
                                              start=(k == 0), stop=(k == KD - 1))
                mm.then_inc(routed, 1)

            def gate_up(n, g, g_par, t, early, width=2 * EG * I):
                if t == 0:
                    pe.wait_ge(w_split, WP * g + KD)
                if early and n in (0, HT):
                    pe.wait_ge(hT_ready, KD * (n // HT + 1))
                if not (early and n < 2):
                    pe.wait_ge(gu_done, n - 1)
                for k in range(KD):
                    mm = product(nc, pgu[:, t % 2, 0:width], [h[:, k, t * P:(t + 1) * P] for h in (hT_hi, hT_lo)],
                                 [w[:, g_par, k, 0:width] for w in (weights_hi, weights_lo)],
                                 start=(k == 0), stop=(k == KD - 1))
                mm.then_inc(gu_ready, 1)

            def turn(n, b, early, width=EG * I):
                pe.wait_ge(a_ready, n + 1)
                if not (early and n < 2):
                    pe.wait_ge(aT_ready, n - 1)
                for k in range(-(-width // P)):
                    m = min(P, width - k * P)
                    mm = nc.tensor.transpose(pat[0:m, b, k * P:(k + 1) * P], act_in[:, b, k * P:k * P + m], ident[:, :])
                mm.then_inc(a_turned, 1)

            def add(n, b, g, t, g_par, early, width=EG * I):
                if t == 0:
                    pe.wait_ge(w_split, WP * (g + 1))
                if early and n == 0:
                    pe.wait_ge(zeroed, 4)
                pe.wait_ge(aT_ready, n + 1)
                for k in range(-(-width // P)):
                    m = min(P, width - k * P)
                    mm = product(nc, pacc[:, t, :], [a[0:m, b, k * P:(k + 1) * P] for a in (aT_hi, aT_lo)],
                                 [w[0:m, g_par, KD, k * D:(k + 1) * D] for w in (weights_hi, weights_lo)],
                                 start=False, stop=False, skip_group_check=True)
                mm.then_inc(added, 1)

            def group(base, g, g_par, early, last=False):
                for t in range(QT):
                    n = base + t
                    gate_up(n, g, g_par, t, early, 2 * I if last else 2 * EG * I)
                    if not (early and n < LAG_T):
                        turn(n - LAG_T, t % 2, early, I if last and t >= LAG_T else EG * I)
                    if not (early and n < LAG_D):
                        same = t >= LAG_D
                        add(n - LAG_D, (t - LAG_D) % 2, g if same else g - 1, (t - LAG_D) % QT,
                            g_par if same else 1 - g_par, early, I if last and same else EG * I)

            group(0, 0, 0, True)
            group(QT, 1, 1, False)
            with pe.Fori(1, NEG // 2) as i:
                for par in range(2):
                    group(2 * QT * i + QT * par, 2 * i + par, par, False)
            group(NEG * QT, NEG, 0, False, last=True)
            for t in range(LAG_D):
                n = NU + t
                if t < LAG_T:
                    turn(n - LAG_T, t % 2, False, I)
                add(n - LAG_D, (n - LAG_D) % 2, NEG, QT - LAG_D + t, 0, False, I)

        @block.scalar
        def _(act):
            act.wait_ge(loaded, 16 * 5)
            nc.scalar.activation(tgates[:, :], gates[:, :], ACT.Tanh).then_inc(tanhs, 1)
            for k in range(KD):
                nc.scalar.activation(wps[:, k, :], wp[:, k, :], ACT.Copy, scale=sv[:, k:k + 1]).then_inc(wp_ready, 1)

            def split_weights(g, par, piece):
                if piece == 0:
                    act.wait_ge(w_in[par], 32 * (g // 2 + 1))
                    if not (isinstance(g, int) and g < 2):
                        act.wait_ge(gu_ready, QT * (g - 1))
                if piece == KD and not (isinstance(g, int) and g < 2):
                    act.wait_ge(added, QT * (g - 1))
                nc.scalar.copy(weights_hi[:, par, piece, :], weights[:, par, piece, :]).then_inc(w_hi, 1)

            for half in range(2):
                cols = slice(half * KC, (half + 1) * KC)
                for k in range(KD):
                    act.wait_ge(turned, KD * half + k + 1)
                    nc.scalar.copy(xT[:, k, cols], wide[:, (2 * half + k) * KC:][:, 0:KC]).then_inc(xT_ready, 1)
            for g in range(2):
                for piece in range(WP):
                    split_weights(g, g, piece)

            def round_rows(half):
                cols = slice(half * KC, (half + 1) * KC)
                for k in range(KD):
                    act.wait_ge(xT_ready, KD * (2 + half) + k + 1)
                    nc.scalar.copy(hT_hi[:, k, cols], xT[:, k, cols]).then_inc(hT_high, 1)

            def exponentials(half):
                ts = slice(HT * half, HT * (half + 1))
                act.wait_ge(shifted, half + 1)
                nc.scalar.activation(probs[:, ts, :], probs[:, ts, :], ACT.Exp).then_inc(exped, 1)
                nc.scalar.activation(sig[:, ts], sig[:, ts], ACT.Tanh, scale=0.5).then_inc(exped, 1)

            for half in range(2):
                act.wait_ge(steps, LN_BASE[half] + VAR_STEP)
                ts = slice(HT * half, HT * (half + 1))
                nc.scalar.activation(ln[:, 1, ts], ln[:, 0, ts], ACT.Sqrt).then_inc(root, 1)
                if half == 1:
                    act.wait_ge(zero_made, 1)
                    nc.scalar.activation(one[:, :], zero[:, :], ACT.Exp).then_inc(one_made, 1)
                cols = slice(half * KC, (half + 1) * KC)
                for k in range(KD):
                    act.wait_ge(turned, KD * (2 + half) + k + 1)
                    nc.scalar.copy(xT[:, k, cols], wide[:, (2 * half + k) * KC:][:, 0:KC]).then_inc(xT_ready, 1)
                if half == 0:
                    round_rows(0)
            exponentials(0)
            round_rows(1)
            exponentials(1)
            act.wait_ge(zero_made, 1)
            for n in range(4):
                nc.scalar.copy(wide[:, n * KC:(n + 1) * KC], zero[:, 0:1].broadcast_to([P, KC])).then_inc(zeroed, 1)

            def tanh(n, b, early, width=EG * I):
                act.wait_ge(gu_ready, n + 1)
                if not (early and n < 2):
                    act.wait_ge(gl_ready, n - 1)
                nc.scalar.activation(th[:, b, 0:width], pgu[:, b, 0:width], ACT.Tanh, scale=0.5).then_inc(th_ready, 1)

            def take(n, b, early, width=EG * I):
                act.wait_ge(a_turned, n + 1)
                if not (early and n < 2):
                    act.wait_ge(added, n - 1)
                m, w = (P, width) if width > P else (width, P)
                nc.scalar.copy(aT_hi[0:m, b, 0:w], pat[0:m, b, 0:w]).then_inc(aT_high, 1)

            def unit(n, g, par, t):
                tanh(n, t % 2, False)
                take(n - 2, t % 2, False)
                if t in SPLIT_AT:
                    split_weights(g + 1, 1 - par, SPLIT_AT.index(t))

            tanh(0, 0, True)
            tanh(1, 1, True)
            for n in range(2, 4):
                tanh(n, n % 2, False)
                take(n - 2, n % 2, True)
            for n in range(4, QT):
                tanh(n, n % 2, False)
                take(n - 2, n % 2, False)
            for t in range(QT):
                unit(QT + t, 1, 1, t)
            with act.Fori(1, NEG // 2) as i:
                for par in range(2):
                    for t in range(QT):
                        unit(2 * QT * i + QT * par + t, 2 * i + par, par, t)
            for n in range(NEG * QT, NU + 2):
                if n < NU:
                    tanh(n, n % 2, False, I)
                take(n - 2, n % 2, False, I if n - 2 >= NEG * QT else EG * I)

        @block.gpsimd
        def _(pool):
            def weigh(n, b, t, col, early, experts=EG):
                pool.wait_ge(gu_done, n + 1)
                if not (early and n < 2):
                    pool.wait_ge(a_turned, n - 1)
                w = experts * I
                nc.gpsimd.tensor_tensor(act_in[:, b, 0:w].rearrange("p (e i) -> p e i", e=experts),
                                        gu[:, b, 0:w].rearrange("p (e i) -> p e i", e=experts),
                                        last_axis(share[:, t, bass.ds(col, experts)], I), ALU.mult).then_inc(a_ready, 1)

            def rest_of(par, piece, g):
                pool.wait_ge(w_hi, WP * g + piece + 1)
                nc.gpsimd.tensor_tensor(weights_lo[:, par, piece, :], weights[:, par, piece, :],
                                        weights_hi[:, par, piece, :].bitcast(F32), ALU.subtract).then_inc(w_split, 1)

            def group(g, par, early=False):
                for t in range(QT):
                    if early and t % HT == 0:
                        pool.wait_ge(share_ready, t // HT + 1)
                    weigh(QT * g + t, t % 2, t, EG * g, early)
                    if t in SPLIT_AT and not early:
                        rest_of(1 - par, SPLIT_AT.index(t), g + 1)

            pool.memset(zero[:, :], 0.0).then_inc(zero_made, 1)
            pool.wait_ge(loaded, 16 * 5)
            pool.wait_ge(tanhs, 1)
            nc.gpsimd.tensor_scalar(bpg[:, :], bp[:, :], tgates[:, 0:1], 0.0, ALU.mult, ALU.add).then_inc(xb_ready, 1)
            pool.wait_ge(xb_ready, 1)
            for half in range(2):
                ts = slice(HT * half, HT * (half + 1))
                nc.gpsimd.tensor_tensor(y[:, ts, :], x[:, ts, :], middle_axis(bpg[:, :], HT),
                                        ALU.add).then_inc(xb_ready, 1)
            for g in range(2):
                for piece in range(WP):
                    rest_of(g, piece, g)
            for half in range(2):
                cols = slice(half * KC, (half + 1) * KC)
                for k in range(KD):
                    pool.wait_ge(hT_high, KD * half + k + 1)
                    nc.gpsimd.tensor_tensor(hT_lo[:, k, cols], xT[:, k, cols], hT_hi[:, k, cols].bitcast(F32),
                                            ALU.subtract).then_inc(hT_ready, 1)
            group(0, 0, True)
            group(1, 1)
            with pool.Fori(1, NEG // 2) as i:
                for par in range(2):
                    group(2 * i + par, par)
            for t in range(QT):
                weigh(NEG * QT + t, t % 2, t, E, False, 1)

        @block.vector
        def _(dve):
            c = Steps(dve, steps)
            c.then(nc.vector.reciprocal(rsum[:, UNITS - 2 * H:], sums[:, UNITS - 2 * H:]))
            over_sums(nc, keep, range(QT - 2, QT)).then_inc(o_ready, 1)
            for half in range(2):
                tiles = range(HT * half, HT * (half + 1))
                ts = slice(HT * half, HT * (half + 1))
                dve.wait_ge(proj, half + 1)
                dve.wait_ge(xb_ready, half + 2)
                c.then(nc.vector.scalar_tensor_tensor(x[:, ts, :], pacc[:, ts, :], tgates[:, 0:1], y[:, ts, :],
                                                      ALU.mult, ALU.add))
                assert c.n == LN_BASE[half]
                layernorm(nc, dve, c, x, stats, mv, ln, on, root, h_ready, tiles, half + 1)

            def route(half):
                ts = slice(HT * half, HT * (half + 1))
                dve.wait_ge(routed, half + 1)
                logits = pat[:, half, :].rearrange("p (t n) -> p t n", n=P)
                c.then(nc.vector.tensor_reduce(lmax[:, ts], logits[:, :, 0:E], AX.X, ALU.max))
                nc.vector.tensor_copy(sig[:, ts], logits[:, :, E])
                nc.vector.tensor_tensor(probs[:, ts, :], logits[:, :, 0:E], last_axis(lmax[:, ts], E),
                                        ALU.subtract).then_inc(shifted, 1)
                dve.wait_ge(exped, 2 * (half + 1))
                c.then(nc.vector.tensor_reduce(psums[:, ts], probs[:, ts, :], AX.X, ALU.add))
                c.then(nc.vector.reciprocal(psums[:, ts], psums[:, ts]))
                c.then(nc.vector.tensor_tensor(probs[:, ts, :], probs[:, ts, :], last_axis(psums[:, ts], E), ALU.mult))
                for t in range(HT * half, HT * (half + 1)):
                    done = nc.vector.max(top[:, t, :], probs[:, t, :])
                c.then(done)
                for t in range(HT * half, HT * (half + 1)):
                    done = nc.vector.match_replace(rest[:, t, :], top[:, t, :], probs[:, t, :], -1.0)
                c.then(done)
                c.then(nc.vector.tensor_reduce(lmax[:, ts], top[:, ts, :], AX.X, ALU.add))
                c.then(nc.vector.reciprocal(lmax[:, ts], lmax[:, ts]))
                c.then(nc.vector.tensor_scalar(lmax[:, ts], lmax[:, ts], 0.5, None, ALU.mult))
                c.then(nc.vector.scalar_tensor_tensor(probs[:, ts, :], rest[:, ts, :], 0.0, probs[:, ts, :],
                                                      ALU.is_lt, ALU.mult))
                nc.vector.tensor_tensor(share[:, ts, 0:E], probs[:, ts, :], last_axis(lmax[:, ts], E), ALU.mult)
                nc.vector.tensor_scalar(share[:, ts, E], sig[:, ts], 1.0, 0.25,
                                        ALU.add, ALU.mult).then_inc(share_ready, 1)

            for half in range(2):
                route(half)

            def times(n, b, early, width=EG * I):
                dve.wait_ge(th_ready, n + 1)
                if not (early and n < 1):
                    dve.wait_ge(gu_done, n)
                nc.vector.scalar_tensor_tensor(gl[:, b, 0:width], th[:, b, 0:width], 1.0, pgu[:, b, 0:width],
                                               ALU.add, ALU.mult).then_inc(gl_ready, 1)
                dve.wait_ge(gl_ready, n + 1)
                if not (early and n < 2):
                    dve.wait_ge(a_ready, n - 1)
                nc.vector.tensor_tensor(gu[:, b, 0:width], gl[:, b, 0:width], pgu[:, b, width:2 * width],
                                        ALU.mult).then_inc(gu_done, 1)

            def rest_of(n, b, early, width=EG * I):
                dve.wait_ge(aT_high, n + 1)
                if not (early and n < 2):
                    dve.wait_ge(added, n - 1)
                m, w = (P, width) if width > P else (width, P)
                nc.vector.tensor_tensor(aT_lo[0:m, b, 0:w], pat[0:m, b, 0:w], aT_hi[0:m, b, 0:w].bitcast(F32),
                                        ALU.subtract).then_inc(aT_ready, 1)

            for n in range(4):
                times(n, n % 2, n < 2)
                if n >= 2:
                    rest_of(n - 2, n % 2, True)
            with dve.Fori(2, NEG * QT // 2) as i:
                for b in range(2):
                    times(2 * i + b, b, False)
                    rest_of(2 * i + b - 2, b, False)

            def output(a, b):
                dve.wait_ge(added, NU - QT + b)
                nc.vector.scalar_tensor_tensor(y[:, a:b, :], pacc[:, a:b, :], tgates[:, 1:2], x[:, a:b, :],
                                               ALU.mult, ALU.add).then_inc(y_ready, 1)

            for n in range(NEG * QT, NU + 2):
                if n < NU:
                    times(n, n % 2, False, I)
                if n == NU + 1:
                    output(*LAST[0])
                rest_of(n - 2, n % 2, False, I if n - 2 >= NEG * QT else EG * I)
            output(*LAST[1])


def program(nc, io):
    with ExitStack() as ctx:
        def sb(name, shape, dt=F32):
            return ctx.enter_context(nc.sbuf_tensor(name, shape, dt))

        keep = {
            "x": sb("x", [P, QT, D]),
            "ident": sb("ident", [P, P]),
            "sq": sb("sq", [P, STEPS, 2]),
            "sv": sb("sv", [P, KD]),
            "v": sb("v", [P, H, VT, HD], BF16),
            "kT": sb("kT", [P, 2, NK], BF16),
            "qT": sb("qT", [P, 2, 2 * P], BF16),
            "rsum": sb("rsum", [P, UNITS]),
            "on": sb("on", [P, QT, D]),
            "wp": sb("wp", [P, KD, D]),
            "bp": sb("bp", [P, D]),
            "gates": sb("gates", [P, 2]),
            "router": sb("router", [P, KD, E + 1]),
            "ffn_loaded": ctx.enter_context(nc.semaphore("ffn_loaded")),
            "heads_in": [ctx.enter_context(nc.semaphore(f"heads_in{j}")) for j in range(2)],
            "o": sb("o", [P, UNITS * HD]),
            "sums": sb("sums", [P, UNITS]),
        }
        scratch = (nc.dram_tensor("kT_parts", (H, QR, NK), BF16, kind="Internal").ap(),
                   nc.dram_tensor("qT_parts", (H, QR, NQ), BF16, kind="Internal").ap())
        projections(nc, io, keep, scratch)
        attention(nc, io, keep, scratch)
        ffn(nc, io, keep)


def kernel(**inputs):
    import numpy as np
    import concourse.bacc as bacc
    from concourse.bass_utils import run_bass_kernel_spmd

    g = {k: np.asarray(a) for k, a in inputs.items()}
    gu = g["L0_ffn_gate_up_proj"].reshape(NEG, EG, 2, I, D)
    arrays = {
        "x": g["x"].reshape(NQ, D),
        "ctxT": g["ctx_2048"].reshape(NK, D).T,
        "eye": np.eye(P, dtype=np.float32),
        "Wq": g["L0_xattn_Wq"], "bq": g["L0_xattn_bq"].reshape(1, D),
        "Wkv": g["L0_xattn_Wkv"], "bkv": g["L0_xattn_bkv"].reshape(1, 2 * D),
        "bv": g["L0_xattn_bkv"][D:].reshape(KD, P).T,
        "Wp": g["L0_xattn_Wp"], "bp": g["L0_xattn_bp"].reshape(1, D),
        "g_xattn": g["g_xattn"].reshape(1, 1), "g_ffn": g["g_ffn"].reshape(1, 1),
        "router": np.concatenate([g["L0_ffn_router_w"], g["L0_ffn_shared_expert_gate_w"]], 0).T,
        "gate_up": gu.transpose(0, 4, 2, 1, 3).reshape(NEG, D, 2 * EG * I),
        "down": g["L0_ffn_down_proj"].transpose(0, 2, 1).reshape(NEG, EG * I, D),
        "shared_gate_up": np.concatenate([g["L0_ffn_shared_gate_w"], g["L0_ffn_shared_up_w"]], 0).T,
        "shared_down": g["L0_ffn_shared_down_w"].T,
    }
    nc = bacc.Bacc("TRN2", target_bir_lowering=False, num_devices=1)
    io, feed = {}, {}
    for name, a in arrays.items():
        feed[f"in_{name}"] = np.ascontiguousarray(a)
        io[name] = nc.dram_tensor(f"in_{name}", a.shape, mybir.dt.from_np(a.dtype), kind="ExternalInput").ap()
    io["out"] = nc.dram_tensor("out_x", (NQ, D), F32, kind="ExternalOutput").ap()
    program(nc, io)
    r = run_bass_kernel_spmd(nc, [feed], core_ids=[0])
    return r.results[0]["out_x"].reshape(4, NQ // 4, D)
```
